# Optimizing a Trainium2 kernel written in Bass

```python
import numpy as np
import jax
import jax.numpy as jnp

def _softmax(x, axis=-1):
    return jax.nn.softmax(x, axis=axis)

def _gelu(x):
    return jax.nn.gelu(x, approximate=True)

def _silu(x):
    return jax.nn.silu(x)

def _sigmoid(x):
    return jax.nn.sigmoid(x)

def _layernorm(x, axis=-1, eps=1e-05):
    m = jnp.mean(x, axis=axis, keepdims=True)
    v = jnp.var(x, axis=axis, keepdims=True)
    return (x - m) / jnp.sqrt(v + eps)

def _scatter_add(tgt, idx, src, axis=0):
    return tgt.at[idx].add(src)

def _segment_sum(src, seg, n):
    return jax.ops.segment_sum(src, seg, n)
kernel_name = 'mk_flamingo_gated_d1_seqx_r4_655735'

def setup_inputs(seed: int=0):
    np.random.seed(seed)
    _w = jnp.asarray

    def _rec_inputs():
        import jax
        import jax.numpy as jnp
        _rk = jax.random.key(seed)
        x = -0.0002928 + 1 * jax.random.normal(jax.random.fold_in(_rk, 1), (8, 112, 512), jnp.float32)
        _lenS = 112 - jax.random.randint(jax.random.fold_in(_rk, 7), (8,), 0, max(1, 112 // 4) + 1, jnp.int32)
        _lenS2 = 375 - jax.random.randint(jax.random.fold_in(_rk, 8), (8,), 0, max(1, 375 // 4) + 1, jnp.int32)
        _ctx_512P = jax.random.normal(jax.random.fold_in(_rk, 11), (8, 16, 128), jnp.float32)
        _ctx_512c = jax.random.dirichlet(jax.random.fold_in(_rk, 511), 0.3 * jnp.ones((16,), jnp.float32), (8, 375))
        _ctx_512t = jnp.einsum('bsk,bkd->bsd', _ctx_512c, _ctx_512P)
        _ctx_512t = _ctx_512t * jax.lax.rsqrt(jnp.mean(jnp.square(_ctx_512t)) + 1e-12) * 0.953939
        ctx_512 = 0.000227908 + 0.99994 * (_ctx_512t + 0.3 * jax.random.normal(jax.random.fold_in(_rk, 611), (8, 375, 128), jnp.float32))
        _g = jax.random.normal(jax.random.fold_in(_rk, 9001), (2, 1), jnp.float32)
        _g = jnp.sign(_g) * jnp.maximum(jnp.abs(_g), 1.0) + (_g == 0) * 1.0
        g_xattn = _g[0]
        g_ffn = _g[1]
        return (x, ctx_512, g_xattn, g_ffn)
    x, ctx_512, g_xattn, g_ffn = _rec_inputs()

    def _L0_xattn_setup():
        import jax, jax.numpy as jnp
        import numpy as np
        B, S, L = (2, 256, 256)
        DIM_Q, H, K, D_C, D_CQ, R = (512, 16, 128, 128, 384, 64)

        def _rope_tables(length, dim):
            inv = 1.0 / 10000.0 ** (jnp.arange(0, dim, 2, dtype=jnp.float32) / dim)
            f = jnp.arange(length, dtype=jnp.float32)[:, None] * inv[None, :]
            sin = jnp.repeat(jnp.sin(f), 2, axis=-1)
            cos = jnp.repeat(jnp.cos(f), 2, axis=-1)
            return (sin, cos)

        def _rotate_half(x):
            half = x.shape[-1] // 2
            return jnp.concatenate([-x[..., half:], x[..., :half]], axis=-1)

        def _apply_rope(x, sin, cos):
            return x * cos + _rotate_half(x) * sin
        key = jax.random.key(seed)
        ks = jax.random.split(key, 8)
        return {'hidden_q': jax.random.normal(ks[0], (B, S, DIM_Q), jnp.float32), 'kv_c': jax.random.normal(ks[1], (B, L, D_C), jnp.float32), 'Wq': jax.random.normal(ks[2], (H * K, DIM_Q), jnp.float32) / np.sqrt(DIM_Q).astype(np.float32), 'w_kc_q': jax.random.normal(ks[3], (H, K, D_CQ), jnp.float32) / np.sqrt(K).astype(np.float32), 'w_kc_kv': jax.random.normal(ks[4], (H, K, D_C), jnp.float32) / np.sqrt(K).astype(np.float32), 'W_qr': jax.random.normal(ks[5], (H, D_CQ, R), jnp.float32) / np.float32(np.sqrt(D_CQ) * np.sqrt(R)), 'W_kr': jax.random.normal(ks[6], (H, D_C, R), jnp.float32) / np.sqrt(D_C).astype(np.float32), 'Wo': jax.random.normal(ks[7], (DIM_Q, H * K), jnp.float32) / np.sqrt(H * K).astype(np.float32)}
    _L0_xattn_all = _L0_xattn_setup()
    _L0_xattn_in = {k: v for k, v in _L0_xattn_all.items() if k in ('Wq', 'w_kc_q', 'w_kc_kv', 'W_qr', 'W_kr', 'Wo')}
    del _L0_xattn_all

    def _L0_ffn_setup():
        import jax, jax.numpy as jnp
        import numpy as np
        B, S, H = (2, 512, 512)
        I = 1024
        E = 8
        TOP_K = 4
        key = jax.random.key(seed)
        k0, k1, k2, k3, k4 = jax.random.split(key, 5)
        scale = 0.02
        return {'hidden_states': jax.random.normal(k0, (B, S, H), dtype=jnp.float32), 'router_w': jax.random.normal(k1, (H, E), dtype=jnp.float32) * scale, 'w1': jax.random.normal(k2, (E, H, I), dtype=jnp.float32) * scale, 'w2': jax.random.normal(k3, (E, I, I), dtype=jnp.float32) * scale, 'w3': jax.random.normal(k4, (E, I, H), dtype=jnp.float32) * scale}
    _L0_ffn_all = _L0_ffn_setup()
    _L0_ffn_in = {k: v for k, v in _L0_ffn_all.items() if k in ('router_w', 'w1', 'w2', 'w3')}
    del _L0_ffn_all
    return {'x': x, 'ctx_512': ctx_512, 'g_xattn': g_xattn, 'g_ffn': g_ffn, 'L0_xattn_Wq': _L0_xattn_in['Wq'], 'L0_xattn_w_kc_q': _L0_xattn_in['w_kc_q'], 'L0_xattn_w_kc_kv': _L0_xattn_in['w_kc_kv'], 'L0_xattn_W_qr': _L0_xattn_in['W_qr'], 'L0_xattn_W_kr': _L0_xattn_in['W_kr'], 'L0_xattn_Wo': _L0_xattn_in['Wo'], 'L0_ffn_router_w': _L0_ffn_in['router_w'], 'L0_ffn_w1': _L0_ffn_in['w1'], 'L0_ffn_w2': _L0_ffn_in['w2'], 'L0_ffn_w3': _L0_ffn_in['w3']}

def reference(x, ctx_512, g_xattn, g_ffn, L0_xattn_Wq, L0_xattn_w_kc_q, L0_xattn_w_kc_kv, L0_xattn_W_qr, L0_xattn_W_kr, L0_xattn_Wo, L0_ffn_router_w, L0_ffn_w1, L0_ffn_w2, L0_ffn_w3):
    import jax
    import jax.numpy as jnp

    def _L0_xattn_ref(hidden_q, kv_c, Wq, w_kc_q, w_kc_kv, W_qr, W_kr, Wo):
        import jax, jax.numpy as jnp
        import numpy as np
        B, S, L = (2, 256, 256)
        DIM_Q, H, K, D_C, D_CQ, R = (512, 16, 128, 128, 384, 64)

        def _rope_tables(length, dim):
            inv = 1.0 / 10000.0 ** (jnp.arange(0, dim, 2, dtype=jnp.float32) / dim)
            f = jnp.arange(length, dtype=jnp.float32)[:, None] * inv[None, :]
            sin = jnp.repeat(jnp.sin(f), 2, axis=-1)
            cos = jnp.repeat(jnp.cos(f), 2, axis=-1)
            return (sin, cos)

        def _rotate_half(x):
            half = x.shape[-1] // 2
            return jnp.concatenate([-x[..., half:], x[..., :half]], axis=-1)

        def _apply_rope(x, sin, cos):
            return x * cos + _rotate_half(x) * sin
        Bv, Sv, _ = hidden_q.shape
        _, Lv, _ = kv_c.shape
        q_hk = (hidden_q @ Wq.T).reshape(Bv, Sv, H, K)
        q_big = jnp.einsum('bshk,hkq->bshq', q_hk, w_kc_q)
        sin_q, cos_q = _rope_tables(Sv, D_CQ)
        q_big = _apply_rope(q_big, sin_q[None, :, None, :], cos_q[None, :, None, :])
        sin_k, cos_k = _rope_tables(Lv, D_C)
        kv_r = _apply_rope(kv_c, sin_k[None], cos_k[None])
        q_r = jnp.einsum('bshq,hqr->bhsr', q_big, W_qr)
        k_r = jnp.einsum('bld,hdr->bhlr', kv_r, W_kr)
        scores = jnp.einsum('bhsr,bhlr->bhsl', q_r, k_r)
        attn = jax.nn.softmax(scores, axis=-1)
        ctx_c = jnp.einsum('bhsl,bld->bhsd', attn, kv_r)
        ctx_lat = jnp.einsum('bhsd,hkd->bhsk', ctx_c, w_kc_kv)
        ctx = ctx_lat.transpose(0, 2, 1, 3).reshape(Bv, Sv, H * K)
        return ctx @ Wo.T

    def _L0_ffn_ref(hidden_states, router_w, w1, w2, w3):
        import jax, jax.numpy as jnp
        import numpy as np
        B, S, H = (2, 512, 512)
        I = 1024
        E = 8
        TOP_K = 4
        b, s, h = hidden_states.shape
        x = hidden_states.reshape(-1, h)
        T = x.shape[0]
        router_logits = x @ router_w
        router_probs = jax.nn.softmax(router_logits, axis=-1)
        top_k_probs, top_k_idx = jax.lax.top_k(router_probs, TOP_K)
        top_k_probs = top_k_probs / jnp.sum(top_k_probs, axis=-1, keepdims=True)
        gates = jnp.zeros((T, E), dtype=x.dtype)
        gates = gates.at[jnp.arange(T)[:, None], top_k_idx].add(top_k_probs)
        h1 = jax.nn.silu(jnp.einsum('th,ehi->eti', x, w1))
        h2 = jax.nn.silu(jnp.einsum('eti,eij->etj', h1, w2))
        out_e = jnp.einsum('etj,ejh->eth', h2, w3)
        out = jnp.einsum('eth,te->th', out_e, gates)
        return out.reshape(b, s, h)
    x = x + jnp.tanh(g_xattn[0]) * _L0_xattn_ref(_layernorm(x, axis=-1), ctx_512, L0_xattn_Wq, L0_xattn_w_kc_q, L0_xattn_w_kc_kv, L0_xattn_W_qr, L0_xattn_W_kr, L0_xattn_Wo)
    x = x + jnp.tanh(g_ffn[0]) * _L0_ffn_ref(_layernorm(x, axis=-1), L0_ffn_router_w, L0_ffn_w1, L0_ffn_w2, L0_ffn_w3)
    return x

_drawn_inputs = setup_inputs


def setup_inputs(seed=0):
    import zlib

    import numpy as np

    out = dict(_drawn_inputs(seed))
    spreads = {}
    factors = {'L0_ffn_router_w': 3.341}
    for name, (base, spread) in spreads.items():
        noise = np.random.default_rng([zlib.crc32(name.encode()), seed]).standard_normal(out[name].shape)
        drawn = base * np.exp(spread * noise) if base else spread * noise
        out[name] = jnp.asarray(drawn.astype(out[name].dtype))
    for name, factor in factors.items():
        out[name] = (out[name] * factor).astype(out[name].dtype)
    return out
```

```python
from contextlib import ExitStack

import numpy as np

import concourse.bass as bass
from concourse import mybir

ALU = mybir.AluOpType
ACT = mybir.ActivationFunctionType
AX_X = mybir.AxisListType.X
F32 = mybir.dt.float32
F32R = mybir.dt.float32r
U32 = mybir.dt.uint32

P = 128
B, S, D = 8, 112, 512
L, DC = 375, 128
LC, LP = 3, 125
LE = 376
H, KH, DQ, R = 16, 128, 384, 64
HQ = 4
NQ = H // HQ
DK = D // P
QC = DQ // P
NC2 = 2
TC = B * S // NC2
EPS = 1e-5


def three_pass(mm, out, lhs_hi, lhs_lo, rhs_hi, rhs_lo, first, last):
    mm(out, lhs_hi, rhs_hi, start=first, stop=False)
    mm(out, lhs_hi, rhs_lo, start=False, stop=False)
    return mm(out, lhs_lo, rhs_hi, start=False, stop=last)


def build_attention(nc, io, keep):
    acc, ident = keep["acc"], keep["ident"]
    with ExitStack() as ctx:
        def sb(name, shape, dt=F32):
            return ctx.enter_context(nc.sbuf_tensor(name, shape, dt))

        def sem(name):
            return ctx.enter_context(nc.semaphore(name))

        def psum(name, shape):
            return ctx.enter_context(nc.psum_tensor(name, shape, F32))

        bank_q = [psum(f"bank_q{i}", [P, 512]) for i in range(2)]
        bank_b = [psum(f"bank_b{i}", [P, 512]) for i in range(3)]
        bank_g = [psum(f"bank_g{i}", [P, 512]) for i in range(2)]
        bank_m = psum("bank_m", [P, 512])

        xnT_hi = sb("xnT_hi", [P, DK, B * S], F32R)
        xnT_lo = sb("xnT_lo", [P, DK, B * S], F32R)
        kvr_hi = sb("kvr_hi", [LP, B * LC, DC], F32R)
        kvr_lo = sb("kvr_lo", [LP, B * LC, DC], F32R)
        kvT_hi = sb("kvT_hi", [P, B, LE], F32R)
        kvT_lo = sb("kvT_lo", [P, B, LE], F32R)
        cos_q = sb("cos_q", [P, QC, S])
        sin_q = sb("sin_q", [P, QC, S])
        stats = sb("stats", [S, B, 6])
        mean_var = sb("mean_var", [S, B, 2])
        rstd = sb("rstd", [S, B])
        eps_col = sb("eps_col", [P, 1])
        gate_col = sb("gate_col", [P, 1])
        tanh_gate = sb("tanh_gate", [P, 1])

        setup = ExitStack()
        xn = setup.enter_context(nc.sbuf_tensor("xn", [S, B, D], F32))
        kv_raw = setup.enter_context(nc.sbuf_tensor("kv_raw", [LP, B * LC, DC], F32))
        kv_rot = setup.enter_context(nc.sbuf_tensor("kv_rot", [LP, B * LC, DC], F32))
        kvr = setup.enter_context(nc.sbuf_tensor("kvr", [LP, B * LC, DC], F32))
        cos_k = setup.enter_context(nc.sbuf_tensor("cos_k", [LP, LC, DC], F32))
        sin_k = setup.enter_context(nc.sbuf_tensor("sin_k", [LP, LC, DC], F32))
        setup.close()

        wq_raw = sb("wq_raw", [P, 2, DK, KH])
        wc_raw = sb("wc_raw", [P, 2, DQ])
        wqr = sb("wqr", [R, 2, DQ + R])
        wkr = sb("wkr", [R, 2, DC])
        wkv = sb("wkv", [KH, 2, DC])
        wo = sb("wo", [KH, 2, D])
        wq_hi = sb("wq_hi", [P, 2, DK, KH], F32R)
        wq_lo = sb("wq_lo", [P, 2, DK, KH], F32R)
        wc_hi = sb("wc_hi", [P, 2, DQ], F32R)
        wc_lo = sb("wc_lo", [P, 2, DQ], F32R)
        m_hi = sb("m_hi", [P, HQ, D], F32R)
        m_lo = sb("m_lo", [P, HQ, D], F32R)
        u_hi = sb("u_hi", [P, HQ, B * S], F32R)
        u_lo = sb("u_lo", [P, HQ, B * S], F32R)
        nmax = sb("nmax", [S, HQ])
        rowsum = sb("rowsum", [S, HQ])
        rinv = sb("rinv", [S, HQ])

        queries = ExitStack()
        qhk_hi = queries.enter_context(nc.sbuf_tensor("qhk_hi", [P, 2, TC], F32R))
        qhk_lo = queries.enter_context(nc.sbuf_tensor("qhk_lo", [P, 2, TC], F32R))
        roped = queries.enter_context(nc.sbuf_tensor("roped", [P, 2, 2 * QC, TC], F32))
        g_mat = queries.enter_context(nc.sbuf_tensor("g_mat", [P, 2, 2 * QC, DC], F32))
        queries.close()
        probs = sb("probs", [S, HQ, L])
        pT_hi = sb("pT_hi", [LP, 2, LC, HQ * S], F32R)
        pT_lo = sb("pT_lo", [LP, 2, LC, HQ * S], F32R)
        cx_hi = sb("cx_hi", [P, 2, HQ * S], F32R)
        cx_lo = sb("cx_lo", [P, 2, HQ * S], F32R)

        x_loaded = sem("x_loaded")
        kv_loaded = sem("kv_loaded")
        const_loaded = sem("const_loaded")
        eps_ready = sem("eps_ready")
        stats_ready = sem("stats_ready")
        mv_ready = sem("mv_ready")
        std_ready = sem("std_ready")
        rstd_ready = sem("rstd_ready")
        xn_ready = sem("xn_ready")
        tanh_ready = sem("tanh_ready")
        rope_step = sem("rope_step")
        kvr_ready = sem("kvr_ready")
        split_hi = sem("split_hi")
        split_done = sem("split_done")
        setup_T = sem("setup_T")
        setup_hi = sem("setup_hi")
        setup_lo = sem("setup_lo")
        pad_ready = sem("pad_ready")
        head_loaded = [sem(f"head_loaded{i}") for i in range(2)]
        w_slot_free = sem("w_slot_free")
        w_step = sem("w_step")
        w_ready = sem("w_ready")
        gm_done = sem("gm_done")
        g_ready = sem("g_ready")
        m_hi_ready = sem("m_hi_ready")
        m_ready = sem("m_ready")
        q_done = sem("q_done")
        q_hi_ready = sem("q_hi_ready")
        q_ready = sem("q_ready")
        lat_done = sem("lat_done")
        rope_ready = sem("rope_ready")
        u_done = sem("u_done")
        u_hi_ready = sem("u_hi_ready")
        u_ready = sem("u_ready")
        sc_done = sem("sc_done")
        max_ready = sem("max_ready")
        exp_ready = sem("exp_ready")
        inv_ready = sem("inv_ready")
        prob_ready = sem("prob_ready")
        pT_done = sem("pT_done")
        pT_hi_ready = sem("pT_hi_ready")
        pT_ready = sem("pT_ready")
        cx_done = sem("cx_done")
        cx_hi_ready = sem("cx_hi_ready")
        cx_ready = sem("cx_ready")
        o_done = sem("o_done")
        acc_ready = sem("acc_ready")

        block = ctx.enter_context(nc.Block())

        HEAD_DMAS = 6 * 16

        @block.sync
        def _(sp):
            for c in range(4):
                sp.dma_start(acc[:, 2 * c:2 * c + 2, :], io["x"].rearrange("(b s) d -> s b d", s=S)[:, 2 * c:2 * c + 2, :]).then_inc(x_loaded, 16)
            sp.dma_start(ident[:], io["ident"]).then_inc(const_loaded, 16)
            sp.dma_start(gate_col[:], io["g_xattn"].partition_broadcast(P)).then_inc(const_loaded, 16)
            sp.dma_start(cos_k[:], io["cos_k"]).then_inc(kv_loaded, 16)
            sp.dma_start(sin_k[:], io["sin_k"]).then_inc(kv_loaded, 16)
            sp.dma_start(kv_raw[:].rearrange("p (b c) d -> p b c d", c=LC),
                         io["ctx"].rearrange("b (c p) d -> p b c d", p=LP)).then_inc(kv_loaded, 16)
            sp.dma_start(cos_q[:], io["cos_q"]).then_inc(const_loaded, 16)
            sp.dma_start(sin_q[:], io["sin_q"]).then_inc(const_loaded, 16)
            sp.wait_ge(setup_lo, B + B)
            sp.wait_ge(split_done, 1)

            def load_head(h, s):
                for dst, name in ((wq_raw, "wq"), (wc_raw, "wc"), (wqr, "wqr"), (wkr, "wkr"), (wkv, "wkv"), (wo, "wo")):
                    sp.dma_start(dst[:, s], io[name][h]).then_inc(head_loaded[s], 16)

            load_head(0, 0)
            load_head(1, 1)
            with sp.Fori(0, H // 2 - 1) as i:
                for s in range(2):
                    sp.wait_ge(w_ready, 2 * (2 * i + s) + 2)
                    sp.sem_inc(w_slot_free, 1)
                    sp.wait_ge(gm_done, 2 * i + s + 1)
                    load_head(2 * i + s + 2, s)

        @block.gpsimd
        def _(pool):
            pool.memset(kvT_hi[:, :, L:LE].bitcast(F32), 0.0).then_inc(pad_ready, 1)
            pool.memset(kvT_lo[:, :, L:LE].bitcast(F32), 0.0).then_inc(pad_ready, 1)

            def split_head(h, s, n, first=False):
                pool.wait_ge(head_loaded[s], HEAD_DMAS * n)
                if not first:
                    pool.wait_ge(lat_done, 2 * QC * (h - 1))
                    pool.sem_inc(w_slot_free, 1)
                pool.tensor_copy(wq_hi[:, s], wq_raw[:, s]).then_inc(w_step, 1)
                pool.tensor_copy(wc_hi[:, s], wc_raw[:, s]).then_inc(w_step, 1)
                pool.wait_ge(w_step, 2 * h + 2)
                pool.tensor_tensor(wq_lo[:, s], wq_raw[:, s], wq_hi[:, s].bitcast(F32), ALU.subtract).then_inc(w_ready, 1)
                pool.tensor_tensor(wc_lo[:, s], wc_raw[:, s], wc_hi[:, s].bitcast(F32), ALU.subtract).then_inc(w_ready, 1)

            for s in range(2):
                split_head(s, s, 1, first=True)
            with pool.Fori(1, H // 2) as i:
                for s in range(2):
                    split_head(2 * i + s, s, i + 1)

        @block.scalar
        def _(act):
            act.wait_ge(const_loaded, 16 * 4)
            nc.scalar.activation(tanh_gate[:], gate_col[:], ACT.Tanh).then_inc(tanh_ready, 1)
            act.wait_ge(eps_ready, 1)
            act.wait_ge(mv_ready, B)
            nc.scalar.activation(rstd[:], mean_var[:, :, 1], ACT.Sqrt, bias=eps_col[0:S]).then_inc(std_ready, 1)
            act.wait_ge(kvr_ready, 1)
            nc.scalar.activation(kvr_hi[:], kvr[:], ACT.Copy).then_inc(split_hi, 1)
            for n in range(B):
                act.wait_ge(setup_T, n + 1)
                nc.scalar.activation(xnT_hi[:, :, n * S:(n + 1) * S], bank_b[n % 3][:, 0:DK * S].rearrange("p (k s) -> p k s", k=DK),
                                     ACT.Copy).then_inc(setup_hi, 1)
            for b in range(B):
                n = B + b
                act.wait_ge(setup_T, n + 1)
                nc.scalar.activation(kvT_hi[:, b, 0:L], bank_b[n % 3][:, 0:L], ACT.Copy).then_inc(setup_hi, 1)

            with act.Fori(0, NQ) as j:
                def g_and_m(k):
                    h = HQ * j + k
                    act.wait_ge(gm_done, h + 1)
                    if k >= 2:
                        act.wait_ge(u_done, 2 * (h - 2) + 2)
                    for i in range(2):
                        last = nc.scalar.activation(g_mat[:, k % 2, i * QC:(i + 1) * QC, :],
                                                    bank_g[i][:, 0:QC * DC].rearrange("p (c d) -> p c d", c=QC), ACT.Copy)
                    last.then_inc(g_ready, 1)
                    nc.scalar.activation(m_hi[:, k, :], bank_m[:, :], ACT.Copy, scale=tanh_gate[:]).then_inc(m_hi_ready, 1)

                act.wait_ge(tanh_ready, 1)
                g_and_m(0)
                for k in range(HQ):
                    h = HQ * j + k
                    for c in range(2):
                        m = 2 * h + c
                        act.wait_ge(q_done, m + 1)
                        nc.scalar.activation(qhk_hi[:, c, :], bank_q[c][:, 0:TC], ACT.Copy).then_inc(q_hi_ready, 1)
                    if k + 1 < HQ:
                        g_and_m(k + 1)
                    for c in range(2):
                        m = 2 * h + c
                        act.wait_ge(u_done, m + 1)
                        nc.scalar.activation(u_hi[:, k, c * TC:(c + 1) * TC], bank_q[c][:, 0:TC], ACT.Copy).then_inc(u_hi_ready, 1)

                def exp(b, hh):
                    n = HQ * (B * j + b) + hh
                    act.wait_ge(max_ready, n + 1)
                    if b:
                        act.wait_ge(pT_done, n - HQ + 1)
                    nc.scalar.activation(probs[:, hh, :], bank_b[(HQ * b + hh) % 3][0:S, 0:L], ACT.Exp, bias=nmax[:, hh:hh + 1],
                                         accum_out=rowsum[:, hh:hh + 1]).then_inc(exp_ready, 1)

                for hh in range(HQ):
                    exp(0, hh)
                def context_hi(b):
                    g = B * j + b
                    act.wait_ge(cx_done, g + 1)
                    if b >= 2:
                        act.wait_ge(o_done, g - 1)
                    nc.scalar.activation(cx_hi[:, b % 2, :], bank_m[:, 0:HQ * S], ACT.Copy).then_inc(cx_hi_ready, 1)

                for b in range(B):
                    g = B * j + b
                    for hh in range(HQ):
                        n = HQ * g + hh
                        act.wait_ge(pT_done, n + 1)
                        if b >= 2 and hh == 0:
                            act.wait_ge(cx_done, g - 1)
                        nc.scalar.activation(pT_hi[:, b % 2, :, hh * S:(hh + 1) * S],
                                             bank_g[hh % 2][0:LP, 0:LC * S].rearrange("p (c s) -> p c s", c=LC), ACT.Copy).then_inc(pT_hi_ready, 1)
                        if b + 1 < B:
                            exp(b + 1, hh)
                        if b and hh == LC - 1:
                            context_hi(b - 1)
                context_hi(B - 1)

        @block.vector
        def _(dve):
            nc.vector.memset(eps_col[:], EPS).then_inc(eps_ready, 1)
            for b in range(B):
                dve.wait_ge(x_loaded, 64)
                nc.vector.bn_stats(stats[:, b, :], acc[:, b, :]).then_inc(stats_ready, 1)
            for b in range(B):
                dve.wait_ge(stats_ready, b + 1)
                nc.vector.bn_aggr(mean_var[:, b, :], stats[:, b, :]).then_inc(mv_ready, 1)
            dve.wait_ge(std_ready, 1)
            nc.vector.reciprocal(rstd[:], rstd[:]).then_inc(rstd_ready, 1)
            dve.wait_ge(rstd_ready, 1)
            for b in range(B):
                nc.vector.tensor_scalar(xn[:, b, :], acc[:, b, :], mean_var[:, b, 0:1], rstd[:, b:b + 1],
                                        ALU.subtract, ALU.mult).then_inc(xn_ready, 1)
            dve.wait_ge(kv_loaded, 48)
            half = DC // 2
            kv4 = kv_raw[:].rearrange("p (b c) d -> p b c d", c=LC)
            rot4 = kv_rot[:].rearrange("p (b c) d -> p b c d", c=LC)
            kvr4 = kvr[:].rearrange("p (b c) d -> p b c d", c=LC)
            for b in range(B):
                nc.vector.tensor_tensor(rot4[:, b, :, 0:half], kv4[:, b, :, half:DC], sin_k[:, :, 0:half], ALU.mult)
                nc.vector.tensor_tensor(rot4[:, b, :, half:DC], kv4[:, b, :, 0:half], sin_k[:, :, half:DC], ALU.mult)
                last = nc.vector.tensor_tensor(kvr4[:, b], kv4[:, b], cos_k[:], ALU.mult)
            last.then_inc(rope_step, 1)
            dve.wait_ge(rope_step, 1)
            nc.vector.tensor_tensor(kvr[:], kvr[:], kv_rot[:], ALU.add).then_inc(kvr_ready, 1)
            for n in range(B):
                dve.wait_ge(setup_hi, n + 1)
                nc.vector.tensor_tensor(xnT_lo[:, :, n * S:(n + 1) * S], bank_b[n % 3][:, 0:DK * S].rearrange("p (k s) -> p k s", k=DK),
                                        xnT_hi[:, :, n * S:(n + 1) * S].bitcast(F32), ALU.subtract).then_inc(setup_lo, 1)
            dve.wait_ge(split_hi, 1)
            dve.wait_ge(kvr_ready, 1)
            nc.vector.tensor_tensor(kvr_lo[:], kvr[:], kvr_hi[:].bitcast(F32), ALU.subtract).then_inc(split_done, 1)
            for b in range(B):
                n = B + b
                dve.wait_ge(setup_hi, n + 1)
                nc.vector.tensor_tensor(kvT_lo[:, b, 0:L], bank_b[n % 3][:, 0:L], kvT_hi[:, b, 0:L].bitcast(F32),
                                        ALU.subtract).then_inc(setup_lo, 1)
            dve.wait_ge(const_loaded, 64)
            dve.wait_ge(tanh_ready, 1)

            with dve.Fori(0, NQ) as j:
                def m_low(k):
                    dve.wait_ge(m_hi_ready, HQ * j + k + 1)
                    nc.vector.scalar_tensor_tensor(out=m_lo[:, k, :], in0=bank_m[:, :], scalar=tanh_gate[:], in1=m_hi[:, k, :].bitcast(F32),
                                                   op0=ALU.mult, op1=ALU.subtract).then_inc(m_ready, 1)

                m_low(0)
                for k in range(HQ):
                    h = HQ * j + k
                    for c in range(2):
                        m = 2 * h + c
                        dve.wait_ge(q_hi_ready, m + 1)
                        nc.vector.tensor_tensor(qhk_lo[:, c, :], bank_q[c][:, 0:TC], qhk_hi[:, c, :].bitcast(F32), ALU.subtract).then_inc(q_ready, 1)
                    for c in range(2):
                        m = 2 * h + c
                        if k:
                            dve.wait_ge(u_done, m - 1)
                        for i in range(QC):
                            dve.wait_ge(lat_done, QC * m + i + 1)
                            lat = bank_b[(QC * c + i) % 3][:, 0:TC].rearrange("p (b s) -> p b s", s=S)
                            for t, table in enumerate((cos_q, sin_q)):
                                last = nc.vector.tensor_tensor(roped[:, c, t * QC + i, :].rearrange("p (b s) -> p b s", s=S), lat,
                                                               table[:, i:i + 1, :].to_broadcast([P, B // 2, S]), ALU.mult)
                            last.then_inc(rope_ready, 1)
                    if k + 1 < HQ:
                        m_low(k + 1)
                    for c in range(2):
                        m = 2 * h + c
                        dve.wait_ge(u_hi_ready, m + 1)
                        nc.vector.tensor_tensor(u_lo[:, k, c * TC:(c + 1) * TC], bank_q[c][:, 0:TC], u_hi[:, k, c * TC:(c + 1) * TC].bitcast(F32),
                                                ALU.subtract).then_inc(u_ready, 1)

                def row_max(b, hh):
                    n = HQ * (B * j + b) + hh
                    dve.wait_ge(sc_done, n + 1)
                    nc.vector.tensor_reduce(nmax[:, hh:hh + 1], bank_b[(HQ * b + hh) % 3][0:S, 0:L], AX_X, ALU.max,
                                            negate=True).then_inc(max_ready, 1)

                def normalise(b, hh):
                    n = HQ * (B * j + b) + hh
                    dve.wait_ge(exp_ready, n + 1)
                    nc.vector.reciprocal(rinv[:, hh:hh + 1], rowsum[:, hh:hh + 1]).then_inc(inv_ready, 1)
                    dve.wait_ge(inv_ready, n + 1)
                    nc.vector.tensor_scalar(probs[:, hh, :], probs[:, hh, :], rinv[:, hh:hh + 1], None, ALU.mult).then_inc(prob_ready, 1)

                def accumulate(b):
                    g = B * j + b
                    dve.wait_ge(o_done, g + 1)
                    nc.vector.tensor_tensor(acc[:, b, :], bank_q[b % 2][0:S, :], acc[:, b, :], ALU.add).then_inc(acc_ready, 1)

                def context_lo(b):
                    dve.wait_ge(cx_hi_ready, B * j + b + 1)
                    nc.vector.tensor_tensor(cx_lo[:, b % 2, :], bank_m[:, 0:HQ * S], cx_hi[:, b % 2, :].bitcast(F32),
                                            ALU.subtract).then_inc(cx_ready, 1)

                row_max(0, 0)
                row_max(0, 1)
                for hh in range(HQ):
                    if hh + 2 < HQ:
                        row_max(0, hh + 2)
                    normalise(0, hh)
                for b in range(B):
                    g = B * j + b
                    for hh in range(HQ):
                        n = HQ * g + hh
                        if b and hh == LC:
                            context_lo(b - 1)
                        if b + 1 < B:
                            row_max(b + 1, hh)
                        dve.wait_ge(pT_hi_ready, n + 1)
                        nc.vector.tensor_tensor(pT_lo[:, b % 2, :, hh * S:(hh + 1) * S],
                                                bank_g[hh % 2][0:LP, 0:LC * S].rearrange("p (c s) -> p c s", c=LC),
                                                pT_hi[:, b % 2, :, hh * S:(hh + 1) * S].bitcast(F32), ALU.subtract).then_inc(pT_ready, 1)
                        if b + 1 < B:
                            normalise(b + 1, hh)
                        if b >= 3 and hh == 0:
                            accumulate(b - 3)
                accumulate(B - 3)
                context_lo(B - 1)
                accumulate(B - 2)
                accumulate(B - 1)

        @block.tensor
        def _(pe):
            mm = nc.tensor.matmul
            pe.wait_ge(const_loaded, 64)
            for n in range(B):
                pe.wait_ge(xn_ready, n + 1)
                if n >= 3:
                    pe.wait_ge(setup_lo, n - 2)
                for k in range(DK):
                    last = nc.tensor.transpose(bank_b[n % 3][:, k * S:(k + 1) * S], xn[:, n, k * P:(k + 1) * P], ident[0:S, 0:S])
                last.then_inc(setup_T, 1)
            pe.wait_ge(kvr_ready, 1)
            for b in range(B):
                n = B + b
                pe.wait_ge(setup_lo, n - 2)
                for c in range(LC):
                    last = nc.tensor.transpose(bank_b[n % 3][:, c * LP:(c + 1) * LP], kvr[:, LC * b + c, :], ident[0:LP, 0:LP])
                last.then_inc(setup_T, 1)
            pe.wait_ge(setup_lo, 2 * B)
            pe.wait_ge(pad_ready, 2)
            pe.wait_ge(split_done, 1)

            with pe.Fori(0, NQ) as j:
                def g_and_m(k):
                    h = HQ * j + k
                    s = k % 2
                    pe.wait_ge(head_loaded[s], HEAD_DMAS * (2 * j + k // 2 + 1))
                    if k:
                        pe.wait_ge(g_ready, h)
                        pe.wait_ge(m_ready, h)
                    for t in range(2):
                        for c in range(QC):
                            at = (c * P + t * DQ // 2) % DQ
                            mm(bank_g[t][:, c * DC:(c + 1) * DC], wqr[:, s, at:at + P], wkr[:, s, :], start=True, stop=True)
                    mm(bank_m[:, :], wkv[:, s, :], wo[:, s, :], start=True, stop=True).then_inc(gm_done, 1)

                g_and_m(0)
                for k in range(HQ):
                    h = HQ * j + k
                    s = k % 2
                    pe.wait_ge(w_ready, 2 * h + 2)
                    for c in range(2):
                        if k:
                            pe.wait_ge(u_ready, 2 * h - 1 + c)
                        for i in range(DK):
                            at = slice(c * TC, (c + 1) * TC)
                            last = three_pass(mm, bank_q[c][:, 0:TC], wq_hi[:, s, i, :], wq_lo[:, s, i, :], xnT_hi[:, i, at], xnT_lo[:, i, at],
                                              i == 0, i == DK - 1)
                        last.then_inc(q_done, 1)
                    for c in range(2):
                        m = 2 * h + c
                        pe.wait_ge(q_ready, m + 1)
                        for i in range(QC):
                            if k or c:
                                pe.wait_ge(rope_ready, QC * m + i - 2)
                            at = slice(i * P, (i + 1) * P)
                            three_pass(mm, bank_b[(QC * c + i) % 3][:, 0:TC], wc_hi[:, s, at], wc_lo[:, s, at], qhk_hi[:, c, :], qhk_lo[:, c, :],
                                       True, True).then_inc(lat_done, 1)
                        if c == 0 and k + 1 < HQ:
                            g_and_m(k + 1)
                    pe.wait_ge(g_ready, h + 1)
                    for c in range(2):
                        m = 2 * h + c
                        pe.wait_ge(rope_ready, QC * m + QC)
                        for i in range(2 * QC):
                            last = mm(bank_q[c][:, 0:TC], g_mat[:, s, i, :], roped[:, c, i, :], start=(i == 0), stop=(i == 2 * QC - 1))
                        last.then_inc(u_done, 1)

                def scores(b, hh):
                    n = HQ * (B * j + b) + hh
                    if HQ * b + hh >= 3:
                        pe.wait_ge(exp_ready, n - 2)
                    at = slice(b * S, (b + 1) * S)
                    three_pass(mm, bank_b[(HQ * b + hh) % 3][0:S, 0:LE], u_hi[:, hh, at], u_lo[:, hh, at], kvT_hi[:, b, :], kvT_lo[:, b, :],
                               True, True).then_inc(sc_done, 1)

                def turn(b, hh):
                    n = HQ * (B * j + b) + hh
                    pe.wait_ge(prob_ready, n + 1)
                    if HQ * b + hh >= 2:
                        pe.wait_ge(pT_ready, n - 1)
                    for c in range(LC):
                        last = nc.tensor.transpose(bank_g[hh % 2][0:LP, c * S:(c + 1) * S], probs[:, hh, c * LP:(c + 1) * LP], ident[0:S, 0:S])
                    last.then_inc(pT_done, 1)

                def attend(b, c):
                    g = B * j + b
                    if c == 0:
                        pe.wait_ge(pT_ready, HQ * g + HQ)
                        if b:
                            pe.wait_ge(cx_ready, g)
                    last = three_pass(mm, bank_m[:, 0:HQ * S], kvr_hi[:, LC * b + c, :], kvr_lo[:, LC * b + c, :],
                                      pT_hi[:, b % 2, c, :], pT_lo[:, b % 2, c, :], c == 0, c == LC - 1)
                    if c == LC - 1:
                        last.then_inc(cx_done, 1)

                def project(b, hh):
                    g = B * j + b
                    if hh == 0:
                        pe.wait_ge(cx_ready, g + 1)
                        if b >= 2:
                            pe.wait_ge(acc_ready, g - 1)
                    at = slice(hh * S, (hh + 1) * S)
                    last = three_pass(mm, bank_q[b % 2][0:S, :], cx_hi[:, b % 2, at], cx_lo[:, b % 2, at], m_hi[:, hh, :], m_lo[:, hh, :],
                                      hh == 0, hh == HQ - 1)
                    if hh == HQ - 1:
                        last.then_inc(o_done, 1)

                pe.wait_ge(u_ready, 2 * HQ * j + 2 * HQ)
                pe.wait_ge(m_ready, HQ * j + HQ)
                for hh in range(HQ):
                    scores(0, hh)
                for b in range(B):
                    for hh in range(HQ):
                        turn(b, hh)
                        if b + 1 < B:
                            scores(b + 1, hh)
                        if b and hh < LC:
                            attend(b - 1, hh)
                        if b >= 2:
                            project(b - 2, hh)
                for hh in range(HQ):
                    project(B - 2, hh)
                    if hh < LC:
                        attend(B - 1, hh)
                for hh in range(HQ):
                    project(B - 1, hh)
                pe.wait_ge(acc_ready, B * j + B)


E = 8
TOPK = 4
FI = 1024
FK = FI // P
CAP = 512
BLK = CAP // P
MAXOVF = TOPK * B * S // (CAP + 1)
NI = E + MAXOVF
NIT = 16
UNIT = 1024
NU = 16
RAW = 4
HOT = 3
AHEAD = 4
RING = 8
ROWS = B * S + CAP


def build_experts(nc, io, out, keep):
    acc, ident = keep["acc"], keep["ident"]
    assert B * S <= 2 * CAP
    with ExitStack() as ctx:
        def sb(name, shape, dt=F32):
            return ctx.enter_context(nc.sbuf_tensor(name, shape, dt))

        def sem(name):
            return ctx.enter_context(nc.semaphore(name))

        def psum(name, shape):
            return ctx.enter_context(nc.psum_tensor(name, shape, F32))

        xn_rows = nc.dram_tensor("xn_rows", [ROWS, D], F32, kind="Internal").ap()
        sum_rows = nc.dram_tensor("sum_rows", [ROWS, D], F32, kind="Internal").ap()

        bank_h = [psum(f"bank_h{i}", [P, 512]) for i in range(3)]
        bank_y = [psum(f"bank_y{i}", [P, 512]) for i in range(BLK)]
        bank_t = psum("bank_t", [P, 512])

        raw = sb("raw", [P, RAW, UNIT])
        w_hi = sb("w_hi", [P, RING, UNIT], F32R)
        w_lo = sb("w_lo", [P, RING, UNIT], F32R)
        iota = sb("iota", [S, CAP])
        pad_row = sb("pad_row", [P, BLK])
        pos_tab = sb("pos_tab", [S, NIT, B])
        row_tab = sb("row_tab", [S, NIT, B, 4], F32R)
        experts = sb("experts", [1, NIT], mybir.dt.int32)
        n_items = sb("n_items", [1, 1], mybir.dt.int32)
        idx_next = sb("idx_next", [P, BLK], U32)
        idx = sb("idx", [P, BLK], U32)
        gate_next = sb("gate_next", [P, BLK])
        gate = sb("gate", [P, BLK])
        lists = sb("lists", [P, BLK, 4])
        row_f = sb("row_f", [P, BLK])

        routing = ExitStack()

        def rb(name, shape, dt=F32):
            return routing.enter_context(nc.sbuf_tensor(name, shape, dt))

        xn2 = rb("xn2", [S, B, D])
        xn2T = rb("xn2T", [P, DK, B * S])
        router = rb("router", [P, DK, E])
        stats = rb("stats2", [S, B, 6])
        mean_var = rb("mean_var2", [S, B, 2])
        rstd = rb("rstd2", [S, B])
        eps_col = rb("eps_col2", [P, 1])
        gate_col = rb("gate_col2", [P, 1])
        tanh_gate = rb("tanh_gate2", [P, 1])
        before = rb("before", [S, E, E])
        upper = rb("upper", [S, S])
        upper_r = rb("upper_r", [S, S], F32R)
        ones = rb("ones", [S, P])
        ones_r = rb("ones_r", [S, P], F32R)
        token_row = rb("token_row", [S, B])
        expert_id = rb("expert_id", [P, E])
        zeros = rb("zeros", [P, D])
        logits = rb("logits", [S, B, E])
        pair = rb("pair", [S, B, E, E])
        pair2 = rb("pair2", [S, B, E, E])
        rank = rb("rank", [S, B, E])
        mask = rb("mask", [S, B, E])
        mask_r = rb("mask_r", [S, B, E], F32R)
        lmax = rb("lmax", [S, B])
        prob = rb("prob", [S, B, E])
        psum_k = rb("psum_k", [S, B])
        gates = rb("gates", [S, B, E])
        posm = rb("posm", [S, B, E])
        count = rb("count", [P, E])
        ovf = rb("ovf", [P, E])
        ovf_pair = rb("ovf_pair", [P, E, E])
        ovf_at = rb("ovf_at", [P, E])
        n_ovf = rb("n_ovf", [P, 1])
        sel = rb("sel", [P, E, E])
        items_f = rb("items_f", [P, NIT])
        gate_tab = rb("gate_tab", [S, NIT, B])
        routing.close()

        onehot = sb("onehot", [S, HOT, CAP], F32R)
        xg = sb("xg", [P, BLK, D])
        xT_hi = sb("xT_hi", [P, DK, CAP], F32R)
        xT_lo = sb("xT_lo", [P, DK, CAP], F32R)
        h_full = sb("h_full", [P, 2, CAP])
        h_hi = [sb(f"h{i}_hi", [P, FK, CAP], F32R) for i in (1, 2)]
        h_lo = [sb(f"h{i}_lo", [P, FK, CAP], F32R) for i in (1, 2)]
        y_sb = sb("y_sb", [P, BLK, D])

        route_loaded = sem("route_loaded")
        rows_stored = sem("rows_stored")
        zeros_ready = sem("zeros_ready")
        eps2_ready = sem("eps2_ready")
        route_step = sem("route_step")
        mv2_ready = sem("mv2_ready")
        std2_ready = sem("std2_ready")
        xn2_ready = sem("xn2_ready")
        tanh2_ready = sem("tanh2_ready")
        xn2T_done = sem("xn2T_done")
        xn2T_ready = sem("xn2T_ready")
        logits_done = sem("logits_done")
        shifted_ready = sem("shifted_ready")
        exp2_ready = sem("exp2_ready")
        mask_ready = sem("mask_ready")
        pos_done = sem("pos_done")
        tables_ready = sem("tables_ready")

        raw_loaded = [sem(f"raw_loaded{i}") for i in range(RAW)]
        unit_hi = sem("unit_hi")
        unit_lo = sem("unit_lo")
        unit_used = sem("unit_used")
        hot_ready = sem("hot_ready")
        hot_used = sem("hot_used")
        list_step = sem("list_step")
        idx_ready = sem("idx_ready")
        gather_begins = sem("gather_begins")
        scatter_begins = sem("scatter_begins")
        load_begins = sem("load_begins")
        gathered = sem("gathered")
        xT_done = sem("xT_done")
        xT_hi_ready = sem("xT_hi_ready")
        xT_ready = sem("xT_ready")
        h_done = sem("h_done")
        h_hi_ready = sem("h_hi_ready")
        h_ready = sem("h_ready")
        y_done = sem("y_done")
        cur_ready = sem("cur_ready")
        y_ready = sem("y_ready")
        scattered = sem("scattered")
        y_free = sem("y_free")
        out_stored = sem("out_stored")

        block = ctx.enter_context(nc.Block())

        TURN_H = (14, 15)
        TURN_W = (12, 13)
        LAG = 2

        def unit_of(m):
            return m // 2 if m < FK else m - FK + 4

        def items_count(eng):
            eng.wait_ge(tables_ready, 1)
            return eng.value_load(n_items[0:1, 0:1], min_val=E, max_val=NI)

        @block.sync
        def _(sp):
            sp.wait_ge(xn2_ready, B)
            sp.dma_start(xn_rows[0:B * S, :].rearrange("(b s) d -> s b d", s=S), xn2[:]).then_inc(rows_stored, 16)
            sp.dma_start(sum_rows[0:B * S, :].rearrange("(b s) d -> s b d", s=S), acc[:]).then_inc(rows_stored, 16)
            sp.wait_ge(zeros_ready, 1)
            for rows in (xn_rows, sum_rows):
                sp.dma_start(rows[B * S:ROWS, :].rearrange("(i p) d -> p i d", p=P), zeros[:].unsqueeze(1).to_broadcast([P, BLK, D])).then_inc(rows_stored, 16)
            items = items_count(sp)

            def load(e, u):
                sp.dma_start(raw[:, u % RAW, :], io["units"][bass.ds(e, 1), u].rearrange("e p n -> (e p) n")).then_inc(raw_loaded[u % RAW], 16)

            for u in range(AHEAD):
                load(0, u)
            with sp.Fori(0, items) as w:
                e = sp.value_load(experts[0:1, bass.ds(w, 1)], min_val=0, max_val=E - 1)
                for u in range(NU - AHEAD):
                    sp.wait_ge(unit_lo, NU * w + u + 1)
                    sp.sem_inc(load_begins, 1)
                    load(e, u + AHEAD)
                e = sp.value_load(experts[0:1, bass.ds(w + 1, 1)], min_val=0, max_val=E - 1)
                for u in range(NU - AHEAD, NU):
                    sp.wait_ge(unit_lo, NU * w + u + 1)
                    sp.sem_inc(load_begins, 1)
                    load(e, u + AHEAD - NU)
            sp.wait_ge(y_free, items + 1)
            sp.sem_inc(load_begins, 1)
            sp.dma_start(out, sum_rows[0:B * S, :]).then_inc(out_stored, 16)
            sp.wait_ge(out_stored, 16)

        @block.gpsimd
        def _(pool):
            pool.memset(zeros[:], 0.0).then_inc(zeros_ready, 1)
            pool.dma_start(iota[:], io["iota"].partition_broadcast(S)).then_inc(route_loaded, 16)
            for dst, name in ((router, "router"), (before, "before"), (upper, "upper"), (ones, "ones"), (token_row, "token_row"),
                              (expert_id, "expert_id"), (pad_row, "pad_row")):
                pool.dma_start(dst[:], io[name]).then_inc(route_loaded, 16)
            pool.dma_start(gate_col[:], io["g_ffn"].partition_broadcast(P)).then_inc(route_loaded, 16)
            pool.sem_inc(y_free, 1)
            items = items_count(pool)
            pool.wait_ge(rows_stored, 64)

            def gather(n):
                pool.wait_ge(idx_ready, n + 1)
                pool.sem_inc(gather_begins, 1)
                for i in range(BLK):
                    pool.indirect_dma_start(xg[:, i, :], None, xn_rows, bass.IndirectOffsetOnAxis(ap=idx_next[:, i:i + 1], axis=0)).then_inc(gathered, 16)

            gather(0)
            with pool.Fori(0, items) as w:
                gather(w + 1)
                pool.wait_ge(y_ready, BLK * w + BLK)
                pool.sem_inc(scatter_begins, 1)
                for i in range(BLK):
                    pool.indirect_dma_start(sum_rows, bass.IndirectOffsetOnAxis(ap=idx[:, i:i + 1], axis=0), y_sb[:, i, :], None,
                                            compute_op=ALU.add).then_inc(scattered, 16)
                pool.wait_ge(scattered, 16 * BLK * (w + 1))
                pool.sem_inc(y_free, 1)

        @block.scalar
        def _(act):
            act.wait_ge(route_loaded, 16 * 9)
            nc.scalar.activation(tanh_gate[:], gate_col[:], ACT.Tanh).then_inc(tanh2_ready, 1)
            act.wait_ge(eps2_ready, 1)
            act.wait_ge(mv2_ready, B)
            nc.scalar.activation(rstd[:], mean_var[:, :, 1], ACT.Sqrt, bias=eps_col[0:S]).then_inc(std2_ready, 1)
            act.wait_ge(shifted_ready, 1)
            nc.scalar.activation(prob[:], prob[:], ACT.Exp).then_inc(exp2_ready, 1)
            items = items_count(act)

            def unit(w, u):
                act.wait_ge(raw_loaded[u % RAW], 16 * ((NU // RAW) * w + u // RAW + 1))
                if AHEAD <= u < RING - 1:
                    act.wait_ge(unit_used, (AHEAD - 1) * w + u - AHEAD + 1)
                elif u == RING - 1:
                    act.wait_ge(y_done, BLK * w + BLK)
                elif RING <= u < RING + 4:
                    act.wait_ge(h_done, 2 * FK * w + 2 * (u - RING) + 2)
                elif u >= RING + 4:
                    act.wait_ge(h_done, 2 * FK * w + FK + u - RING - 4 + 1)
                nc.scalar.activation(w_hi[:, u % RING, :], raw[:, u % RAW, :], ACT.Copy).then_inc(unit_hi, 1)

            def turned(n, i):
                act.wait_ge(xT_done, BLK * n + i + 1)
                nc.scalar.activation(xT_hi[:, :, i * P:(i + 1) * P], bank_t[:, :].rearrange("p (k s) -> p k s", k=DK), ACT.Copy).then_inc(xT_hi_ready, 1)

            for u in range(AHEAD):
                unit(0, u)
            for i in range(BLK):
                turned(0, i)
            with act.Fori(0, items) as w:
                for m in range(2 * FK):
                    n = 2 * FK * w + m
                    act.wait_ge(h_done, n + 1)
                    if m >= 2:
                        act.wait_ge(h_ready, n - 1)
                    nc.scalar.activation(h_full[:, m % 2, :], bank_h[m % 3][:, :], ACT.Silu)
                    nc.scalar.activation(h_hi[m // FK][:, m % FK, :], bank_h[m % 3][:, :], ACT.Silu).then_inc(h_hi_ready, 1)
                    if m >= FK or m % 2:
                        unit(w, AHEAD + unit_of(m))
                    if m in TURN_H:
                        turned(w + 1, TURN_H.index(m))
                for u in range(NU - 4, NU):
                    unit(w, AHEAD + u)
                    if u in TURN_W:
                        turned(w + 1, len(TURN_H) + TURN_W.index(u))
                act.wait_ge(cur_ready, w + 1)
                for i in range(BLK):
                    act.wait_ge(y_done, BLK * w + i + 1 + BLK)
                    if i == 0:
                        act.wait_ge(y_free, w + 1)
                    nc.scalar.activation(y_sb[:, i, :], bank_y[i][:, :], ACT.Copy, scale=gate[:, i:i + 1]).then_inc(y_ready, 1)

        @block.vector
        def _(dve):
            v = nc.vector
            steps = [0]

            def then(ins):
                steps[0] += 1
                ins.then_inc(route_step, 1)
                dve.wait_ge(route_step, steps[0])

            v.memset(eps_col[:], EPS).then_inc(eps2_ready, 1)
            for b in range(B):
                last = v.bn_stats(stats[:, b, :], acc[:, b, :])
            then(last)
            for b in range(B):
                v.bn_aggr(mean_var[:, b, :], stats[:, b, :]).then_inc(mv2_ready, 1)
            dve.wait_ge(std2_ready, 1)
            then(v.reciprocal(rstd[:], rstd[:]))
            dve.wait_ge(mv2_ready, B)
            for b in range(B):
                v.tensor_scalar(xn2[:, b, :], acc[:, b, :], mean_var[:, b, 0:1], rstd[:, b:b + 1], ALU.subtract, ALU.mult).then_inc(xn2_ready, 1)
            dve.wait_ge(route_loaded, 16 * 9)
            v.tensor_copy(upper_r[:], upper[:])
            v.tensor_copy(ones_r[:], ones[:])
            for b in range(B):
                dve.wait_ge(xn2T_done, b + 1)
                v.tensor_copy(xn2T[:, :, b * S:(b + 1) * S], bank_h[b % 3][:, 0:DK * S].rearrange("p (k s) -> p k s", k=DK)).then_inc(xn2T_ready, 1)
            dve.wait_ge(logits_done, 1)
            then(v.tensor_copy(logits[:], bank_t[0:S, 0:B * E].rearrange("s (b e) -> s b e", e=E)))
            other = logits[:].unsqueeze(2).to_broadcast([S, B, E, E])
            own = logits[:].unsqueeze(3).to_broadcast([S, B, E, E])
            v.tensor_tensor(pair[:], other, own, ALU.is_gt)
            then(v.tensor_tensor(pair2[:], other, own, ALU.is_equal))
            then(v.tensor_tensor(pair2[:], pair2[:], before[:].unsqueeze(1).to_broadcast([S, B, E, E]), ALU.mult))
            then(v.tensor_tensor(pair[:], pair[:], pair2[:], ALU.add))
            then(v.tensor_reduce(rank[:], pair[:], AX_X, ALU.add))
            v.tensor_scalar(mask_r[:], rank[:], float(TOPK), None, ALU.is_lt).then_inc(mask_ready, 1)
            then(v.tensor_scalar(mask[:], rank[:], float(TOPK), None, ALU.is_lt))
            then(v.tensor_reduce(lmax[:], logits[:], AX_X, ALU.max))
            v.tensor_tensor(prob[:], logits[:], lmax[:].unsqueeze(2).to_broadcast([S, B, E]), ALU.subtract).then_inc(shifted_ready, 1)
            dve.wait_ge(exp2_ready, 1)
            then(v.tensor_tensor(prob[:], prob[:], mask[:], ALU.mult))
            then(v.tensor_reduce(psum_k[:], prob[:], AX_X, ALU.add))
            then(v.reciprocal(psum_k[:], psum_k[:]))
            then(v.tensor_tensor(gates[:], prob[:], psum_k[:].unsqueeze(2).to_broadcast([S, B, E]), ALU.mult))
            dve.wait_ge(tanh2_ready, 1)
            then(v.tensor_scalar(gates[:], gates[:], tanh_gate[0:S], None, ALU.mult))
            dve.wait_ge(pos_done, 1)
            then(v.tensor_scalar(posm[:], bank_t[0:S, B * E:2 * B * E].rearrange("s (b e) -> s b e", e=E), 1.0, None, ALU.add))
            then(v.tensor_tensor(posm[:], posm[:], mask[:], ALU.mult))
            then(v.tensor_copy(count[:], bank_t[:, 2 * B * E:2 * B * E + E]))
            then(v.tensor_scalar(ovf[:], count[:], float(CAP), None, ALU.is_gt))
            then(v.tensor_tensor(ovf_pair[0:S], before[:], ovf[0:S].unsqueeze(1).to_broadcast([S, E, E]), ALU.mult))
            then(v.tensor_reduce(ovf_at[0:S], ovf_pair[0:S], AX_X, ALU.add))
            then(v.tensor_tensor(sel[0:S], ovf_at[0:S].unsqueeze(1).to_broadcast([S, E, E]),
                                 expert_id[0:S].unsqueeze(2).to_broadcast([S, E, E]), ALU.is_equal))
            then(v.tensor_tensor(sel[0:S], sel[0:S], ovf[0:S].unsqueeze(1).to_broadcast([S, E, E]), ALU.mult))
            then(v.memset(pos_tab[:], -1.0))
            then(v.memset(gate_tab[:], 0.0))
            then(v.memset(items_f[:], 0.0))
            v.tensor_scalar(pos_tab[:, 0:E, :], posm[:].rearrange("s b e -> s e b"), -1.0, None, ALU.add)
            v.tensor_copy(gate_tab[:, 0:E, :], gates[:].rearrange("s b e -> s e b"))
            then(v.tensor_copy(items_f[0:S, 0:E], expert_id[0:S]))
            pick = sel[0:S].unsqueeze(1).to_broadcast([S, B, E, E])
            then(v.tensor_tensor(pair[:], pick, posm[:].unsqueeze(2).to_broadcast([S, B, E, E]), ALU.mult))
            then(v.tensor_reduce(rank[:], pair[:], AX_X, ALU.add))
            then(v.tensor_scalar(pos_tab[:, E:2 * E, :], rank[:].rearrange("s b q -> s q b"), -1.0 - CAP, None, ALU.add))
            then(v.tensor_tensor(pair[:], pick, gates[:].unsqueeze(2).to_broadcast([S, B, E, E]), ALU.mult))
            then(v.tensor_reduce(rank[:], pair[:], AX_X, ALU.add))
            then(v.tensor_copy(gate_tab[:, E:2 * E, :], rank[:].rearrange("s b q -> s q b")))
            then(v.tensor_tensor(ovf_pair[0:S], sel[0:S], expert_id[0:S].unsqueeze(1).to_broadcast([S, E, E]), ALU.mult))
            then(v.tensor_reduce(items_f[0:S, E:2 * E], ovf_pair[0:S], AX_X, ALU.add))
            v.tensor_copy(experts[:], items_f[0:1, :])
            then(v.tensor_reduce(n_ovf[:], ovf[:], AX_X, ALU.add))
            then(v.tensor_scalar(n_items[:], n_ovf[0:1, :], float(E), None, ALU.add))
            v.tensor_copy(row_tab[:, :, :, 0], token_row[:].unsqueeze(1).to_broadcast([S, NIT, B]))
            v.tensor_scalar(row_tab[:, :, :, 1], gate_tab[:], 0.0, 1.0, ALU.mult, ALU.add)
            then(v.tensor_copy(row_tab[:, :, :, 2], gate_tab[:]))
            v.tensor_tensor(row_tab[:, :, :, 3], gate_tab[:], row_tab[:, :, :, 2].bitcast(F32), ALU.subtract).then_inc(tables_ready, 1)
            items = items_count(dve)

            def unit(w, u):
                dve.wait_ge(unit_hi, NU * w + u + 1)
                v.tensor_tensor(w_lo[:, u % RING, :], raw[:, u % RAW, :], w_hi[:, u % RING, :].bitcast(F32), ALU.subtract).then_inc(unit_lo, 1)

            def hot(n, b):
                dve.wait_ge(hot_used, B * n + b + 1)
                v.tensor_scalar(onehot[:, b % HOT, :], iota[:], pos_tab[:, bass.ds(n, 1), b], None, ALU.is_equal).then_inc(hot_ready, 1)

            def make_list(n):
                dve.wait_ge(hot_used, B * n + B + HOT)
                v.tensor_copy(lists[:], bank_t[:, 0:BLK * 4].rearrange("p (i c) -> p i c", c=4)).then_inc(list_step, 1)
                dve.wait_ge(list_step, 4 * n + 1)
                v.tensor_scalar(row_f[:], lists[:, :, 1], -1.0, 1.0, ALU.mult, ALU.add).then_inc(list_step, 1)
                dve.wait_ge(list_step, 4 * n + 2)
                v.tensor_tensor(row_f[:], row_f[:], pad_row[:], ALU.mult).then_inc(list_step, 1)
                dve.wait_ge(list_step, 4 * n + 3)
                v.tensor_tensor(idx_next[:], row_f[:], lists[:, :, 0], ALU.add).then_inc(idx_ready, 1)
                v.tensor_tensor(gate_next[:], lists[:, :, 2], lists[:, :, 3], ALU.add).then_inc(list_step, 1)

            def turned(n, i):
                dve.wait_ge(xT_hi_ready, BLK * n + i + 1)
                at = slice(i * P, (i + 1) * P)
                v.tensor_tensor(xT_lo[:, :, at], bank_t[:, :].rearrange("p (k s) -> p k s", k=DK), xT_hi[:, :, at].bitcast(F32),
                                ALU.subtract).then_inc(xT_ready, 1)

            for u in range(AHEAD):
                unit(0, u)
            for b in range(B):
                hot(0, b)
            make_list(0)
            for i in range(BLK):
                turned(0, i)
            with dve.Fori(0, items) as w:
                for m in range(2 * FK):
                    dve.wait_ge(h_hi_ready, 2 * FK * w + m + 1)
                    v.tensor_tensor(h_lo[m // FK][:, m % FK, :], h_full[:, m % 2, :], h_hi[m // FK][:, m % FK, :].bitcast(F32),
                                    ALU.subtract).then_inc(h_ready, 1)
                    if m >= FK or m % 2:
                        unit(w, AHEAD + unit_of(m))
                    if m == FK // 2:
                        dve.wait_ge(y_free, w + 1)
                        dve.wait_ge(list_step, 4 * w + 4)
                        v.tensor_copy(idx[:], idx_next[:])
                        v.tensor_copy(gate[:], gate_next[:]).then_inc(cur_ready, 1)
                    if m < B:
                        hot(w + 1, m)
                    if m == B + LAG:
                        dve.wait_ge(cur_ready, w + 1)
                        make_list(w + 1)
                    if m in TURN_H:
                        turned(w + 1, TURN_H.index(m))
                for u in range(NU - 4, NU):
                    unit(w, AHEAD + u)
                    if u in TURN_W:
                        turned(w + 1, len(TURN_H) + TURN_W.index(u))

        @block.tensor
        def _(pe):
            mm = nc.tensor.matmul
            for b in range(B):
                pe.wait_ge(xn2_ready, b + 1)
                if b >= 3:
                    pe.wait_ge(xn2T_ready, b - 2)
                for k in range(DK):
                    last = nc.tensor.transpose(bank_h[b % 3][:, k * S:(k + 1) * S], xn2[:, b, k * P:(k + 1) * P], ident[0:S, 0:S])
                last.then_inc(xn2T_done, 1)
            pe.wait_ge(route_loaded, 16 * 9)
            for b in range(B):
                pe.wait_ge(xn2T_ready, b + 1)
                for k in range(DK):
                    last = mm(bank_t[0:S, b * E:(b + 1) * E], xn2T[:, k, b * S:(b + 1) * S], router[:, k, :], start=(k == 0), stop=(k == DK - 1))
            last.then_inc(logits_done, 1)
            pe.wait_ge(mask_ready, 1)
            pos = bank_t[0:S, B * E:2 * B * E]
            flat = mask_r[:].rearrange("s b e -> s (b e)")
            mm(pos, upper_r[:], flat, start=True, stop=False, skip_group_check=True)
            for d in range(1, B):
                mm(pos[:, d * E:], ones_r[:, 0:S], flat[:, 0:(B - d) * E], start=False, stop=(d == B - 1), skip_group_check=True)
            for b in range(B):
                last = mm(bank_t[:, 2 * B * E:2 * B * E + E], ones_r[:], mask_r[:, b, :], start=(b == 0), stop=(b == B - 1), skip_group_check=True)
            last.then_inc(pos_done, 1)
            pe.sem_inc(unit_used, AHEAD - 1)
            pe.sem_inc(y_done, BLK)
            pe.sem_inc(hot_used, HOT)
            items = items_count(pe)

            def lists_of(n, b):
                pe.wait_ge(hot_ready, B * n + b + 1)
                for i in range(BLK):
                    last = mm(bank_t[:, 4 * i:4 * i + 4], onehot[:, b % HOT, i * P:(i + 1) * P],
                              row_tab[:, bass.ds(n, 1), b, :].rearrange("s o c -> s (o c)"),
                              start=(b == 0 and i == 0), stop=(b == B - 1), skip_group_check=True)
                last.then_inc(hot_used, 1)

            def turn(n, i):
                if i:
                    pe.wait_ge(xT_ready, BLK * n + i)
                pe.wait_ge(gathered, 16 * BLK * (n + 1))
                for k in range(DK):
                    last = nc.tensor.transpose(bank_t[:, k * P:(k + 1) * P], xg[:, i, k * P:(k + 1) * P], ident[:])
                last.then_inc(xT_done, 1)

            for b in range(B):
                lists_of(0, b)
            for i in range(BLK):
                turn(0, i)
            with pe.Fori(0, items) as w:
                pe.wait_ge(xT_ready, BLK * w + BLK)
                for m in range(2 * FK):
                    layer2 = m >= FK
                    n = 2 * FK * w + m
                    u = unit_of(m)
                    pe.wait_ge(unit_lo, NU * w + u + 1)
                    if m >= 3:
                        pe.wait_ge(h_ready, n - 2)
                    kk = FK if layer2 else DK
                    for k in range(kk):
                        if m == FK:
                            pe.wait_ge(h_ready, 2 * FK * w + k + 1)
                        at = slice(k * P, k * P + P) if layer2 else slice(k * 2 * P + (m % 2) * P, k * 2 * P + (m % 2) * P + P)
                        src_hi = h_hi[0][:, k, :] if layer2 else xT_hi[:, k, :]
                        src_lo = h_lo[0][:, k, :] if layer2 else xT_lo[:, k, :]
                        last = three_pass(mm, bank_h[m % 3][:, :], w_hi[:, u % RING, at], w_lo[:, u % RING, at], src_hi, src_lo,
                                          k == 0, k == kk - 1)
                    last.then_inc(h_done, 1)
                    if LAG <= m < B + LAG:
                        lists_of(w + 1, m - LAG)
                    if m in TURN_H:
                        turn(w + 1, TURN_H.index(m))
                for u in range(12, NU):
                    pe.wait_ge(unit_lo, NU * w + u + 1)
                    for i in range(BLK):
                        for c in range(2):
                            k = 2 * (u - 12) + c
                            if i == 0:
                                pe.wait_ge(h_ready, 2 * FK * w + FK + k + 1)
                            at = slice(c * D, (c + 1) * D)
                            tok = slice(i * P, (i + 1) * P)
                            last = three_pass(mm, bank_y[i][:, :], h_hi[1][:, k, tok], h_lo[1][:, k, tok], w_hi[:, u % RING, at], w_lo[:, u % RING, at],
                                              k == 0, k == FK - 1)
                        if u == NU - 1:
                            last.then_inc(y_done, 1)
                    if u < NU - 1:
                        last.then_inc(unit_used, 1)
                    if u in TURN_W:
                        turn(w + 1, len(TURN_H) + TURN_W.index(u))


def rope_tables(length, dim):
    inv = (np.float32(1.0) / np.float32(10000.0) ** (np.arange(0, dim, 2, dtype=np.float32) / np.float32(dim))).astype(np.float32)
    f = np.arange(length, dtype=np.float32)[:, None] * inv[None, :]
    return np.repeat(np.cos(f), 2, axis=-1), np.repeat(np.sin(f), 2, axis=-1)


def constants():
    cq, sq = rope_tables(S, DQ)
    turned = np.roll(sq, -(DQ // 2), axis=1).copy()
    turned[:, DQ // 2:] *= -1
    ck, sk = rope_tables(L, DC)
    sk = sk.copy()
    sk[:, :DC // 2] *= -1
    return {
        "cos_q": cq.T.reshape(QC, P, S).transpose(1, 0, 2), "sin_q": turned.T.reshape(QC, P, S).transpose(1, 0, 2),
        "cos_k": ck.reshape(LC, LP, DC).transpose(1, 0, 2), "sin_k": sk.reshape(LC, LP, DC).transpose(1, 0, 2),
        "ident": np.eye(P, dtype=np.float32),
        "iota": np.arange(CAP, dtype=np.float32), "before": np.broadcast_to(np.tri(E, E, -1, dtype=np.float32), (S, E, E)),
        "upper": np.tri(S, S, -1, dtype=np.float32).T, "ones": np.ones((S, P), np.float32),
        "token_row": (np.arange(S, dtype=np.float32)[:, None] + np.float32(S) * np.arange(B, dtype=np.float32)[None, :]),
        "expert_id": np.broadcast_to(np.arange(E, dtype=np.float32), (P, E)),
        "pad_row": np.float32(B * S) + np.arange(CAP, dtype=np.float32).reshape(BLK, P).T,
    }


def layouts(x):
    wqrT = x["L0_xattn_W_qr"].transpose(0, 2, 1)
    return {
        "x": x["x"].reshape(B * S, D), "ctx": x["ctx_512"], "g_xattn": x["g_xattn"], "g_ffn": x["g_ffn"],
        "wq": x["L0_xattn_Wq"].reshape(H, KH, DK, P).transpose(0, 3, 2, 1),
        "wc": x["L0_xattn_w_kc_q"],
        "wqr": np.concatenate([wqrT, wqrT[:, :, :R]], axis=2),
        "wkr": x["L0_xattn_W_kr"].transpose(0, 2, 1),
        "wkv": x["L0_xattn_w_kc_kv"],
        "wo": x["L0_xattn_Wo"].T.reshape(H, KH, D),
        "router": x["L0_ffn_router_w"].reshape(DK, P, E).transpose(1, 0, 2),
        "units": np.concatenate([
            x["L0_ffn_w1"].reshape(E, DK, P, 4, 2 * P).transpose(0, 3, 2, 1, 4).reshape(E, 4, P, UNIT),
            x["L0_ffn_w2"].reshape(E, FK, P, FK, P).transpose(0, 3, 2, 1, 4).reshape(E, FK, P, UNIT),
            x["L0_ffn_w3"].reshape(E, 4, 2, P, D).transpose(0, 1, 3, 2, 4).reshape(E, 4, P, UNIT)], axis=1),
    }


def program(nc, io, out):
    with nc.sbuf_tensor("acc", [S, B, D], F32) as acc, nc.sbuf_tensor("ident", [P, P], F32) as ident:
        keep = {"acc": acc, "ident": ident}
        build_attention(nc, io, keep)
        build_experts(nc, io, out, keep)


def kernel(**inputs):
    import concourse.bacc as bacc
    from concourse.bass_utils import run_bass_kernel_spmd as run

    x = {name: np.asarray(a) for name, a in inputs.items()}
    nc = bacc.Bacc("TRN2", target_bir_lowering=False, num_devices=1)
    arrays, io = {}, {}
    for name, a in (layouts(x) | constants()).items():
        arrays["in_" + name] = np.ascontiguousarray(a)
        io[name] = nc.dram_tensor("in_" + name, a.shape, F32, kind="ExternalInput").ap()
    out = nc.dram_tensor("out_x", [B * S, D], F32, kind="ExternalOutput").ap()
    program(nc, io, out)
    r = run(nc, [arrays], core_ids=[0])
    return r.results[0]["out_x"].reshape(B, S, D)
```

```python
from contextlib import ExitStack

import numpy as np

import concourse.bass as bass
from concourse import mybir

ALU = mybir.AluOpType
ACT = mybir.ActivationFunctionType
AX_X = mybir.AxisListType.X
F32 = mybir.dt.float32
F32R = mybir.dt.float32r
U32 = mybir.dt.uint32

P = 128
B, S, D = 8, 112, 512
L, DC = 375, 128
LC, LP = 3, 125
LE = 376
H, KH, DQ, R = 16, 128, 384, 64
HQ = 4
NQ = H // HQ
DK = D // P
QC = DQ // P
NC2 = 2
TC = B * S // NC2
EPS = 1e-5


def three_pass(mm, out, lhs_hi, lhs_lo, rhs_hi, rhs_lo, first, last):
    mm(out, lhs_hi, rhs_hi, start=first, stop=False)
    mm(out, lhs_hi, rhs_lo, start=False, stop=False)
    return mm(out, lhs_lo, rhs_hi, start=False, stop=last)


def build_attention(nc, io, keep):
    acc, ident, ffn_gate = keep["acc"], keep["ident"], keep["ffn_gate"]
    with ExitStack() as ctx:
        def sb(name, shape, dt=F32):
            return ctx.enter_context(nc.sbuf_tensor(name, shape, dt))

        def sem(name):
            return ctx.enter_context(nc.semaphore(name))

        def psum(name, shape):
            return ctx.enter_context(nc.psum_tensor(name, shape, F32))

        bank_q = [psum(f"bank_q{i}", [P, 512]) for i in range(2)]
        bank_b = [psum(f"bank_b{i}", [P, 512]) for i in range(3)]
        bank_g = [psum(f"bank_g{i}", [P, 512]) for i in range(2)]
        bank_m = psum("bank_m", [P, 512])

        xnT_hi = sb("xnT_hi", [P, DK, B * S], F32R)
        xnT_lo = sb("xnT_lo", [P, DK, B * S], F32R)
        kvr_hi = sb("kvr_hi", [LP, B * LC, DC], F32R)
        kvr_lo = sb("kvr_lo", [LP, B * LC, DC], F32R)
        kvT_hi = sb("kvT_hi", [P, B, LE], F32R)
        kvT_lo = sb("kvT_lo", [P, B, LE], F32R)
        cos_q = sb("cos_q", [P, QC, S])
        sin_q = sb("sin_q", [P, QC, S])
        stats = sb("stats", [S, B, 6])
        mean_var = sb("mean_var", [S, B, 2])
        rstd = sb("rstd", [S, B])
        eps_col = sb("eps_col", [P, 1])
        gate_col = sb("gate_col", [P, 1])
        tanh_gate = sb("tanh_gate", [P, 1])

        wq_raw = sb("wq_raw", [P, 2, DK, KH])
        wc_raw = sb("wc_raw", [P, 2, DQ])
        wqr = sb("wqr", [R, 2, DQ])
        wkr = sb("wkr", [R, 2, DC])
        wkv = sb("wkv", [KH, 2, DC])
        wo = sb("wo", [KH, 2, D])
        wq_hi = sb("wq_hi", [P, 2, DK, KH], F32R)
        wq_lo = sb("wq_lo", [P, 2, DK, KH], F32R)
        wc_hi = sb("wc_hi", [P, 2, DQ], F32R)
        wc_lo = sb("wc_lo", [P, 2, DQ], F32R)

        setup = ExitStack()
        xn = setup.enter_context(nc.sbuf_tensor("xn", [S, B, D], F32))
        kvr = setup.enter_context(nc.sbuf_tensor("kvr", [LP, B * LC, DC], F32))
        kv_raw = setup.enter_context(nc.sbuf_tensor("kv_raw", [LP, B * LC, DC], F32))
        kv_rot = setup.enter_context(nc.sbuf_tensor("kv_rot", [LP, B * LC, DC], F32))
        cos_k = setup.enter_context(nc.sbuf_tensor("cos_k", [LP, LC, DC], F32))
        sin_k = setup.enter_context(nc.sbuf_tensor("sin_k", [LP, LC, DC], F32))
        setup.close()

        m_hi = sb("m_hi", [P, HQ, D], F32R)
        m_lo = sb("m_lo", [P, HQ, D], F32R)
        u_hi = sb("u_hi", [P, HQ, B * S], F32R)
        u_lo = sb("u_lo", [P, HQ, B * S], F32R)
        nmax = sb("nmax", [S, HQ])
        rowsum = sb("rowsum", [S, HQ])
        rinv = sb("rinv", [S, HQ])

        probs = sb("probs", [S, HQ, L])

        queries = ExitStack()
        qhk_hi = queries.enter_context(nc.sbuf_tensor("qhk_hi", [P, 2, TC], F32R))
        qhk_lo = queries.enter_context(nc.sbuf_tensor("qhk_lo", [P, 2, TC], F32R))
        roped = queries.enter_context(nc.sbuf_tensor("roped", [P, 2, QC, TC], F32))
        turned = queries.enter_context(nc.sbuf_tensor("turned", [P, 2, QC, TC], F32))
        g_mat = queries.enter_context(nc.sbuf_tensor("g_mat", [P, 2, QC, DC], F32))
        queries.close()
        pT_hi = sb("pT_hi", [LP, 2, LC, HQ * S], F32R)
        pT_lo = sb("pT_lo", [LP, 2, LC, HQ * S], F32R)
        cx_hi = sb("cx_hi", [P, 2, HQ * S], F32R)
        cx_lo = sb("cx_lo", [P, 2, HQ * S], F32R)

        x_loaded = [sem(f"x_loaded{c}") for c in range(4)]
        gate_loaded = sem("gate_loaded")
        ident_loaded = sem("ident_loaded")
        kv_loaded = sem("kv_loaded")
        const_loaded = sem("const_loaded")
        eps_ready = sem("eps_ready")
        stats_ready = sem("stats_ready")
        mv_ready = sem("mv_ready")
        std_ready = sem("std_ready")
        rstd_ready = sem("rstd_ready")
        xn_ready = sem("xn_ready")
        tanh_ready = sem("tanh_ready")
        rope_step = [sem("rope_step_dve"), sem("rope_step_pool")]
        kvr_ready = [sem("kvr_ready_dve"), sem("kvr_ready_pool")]
        kvr_hi_ready = sem("kvr_hi_ready")
        kvr_lo_ready = sem("kvr_lo_ready")
        setup_T = sem("setup_T")
        setup_hi = sem("setup_hi")
        setup_lo = sem("setup_lo")
        pad_ready = sem("pad_ready")
        head_loaded = [sem(f"head_loaded{i}") for i in range(2)]
        w_slot_free = sem("w_slot_free")
        w_hi_ready = sem("w_hi_ready")
        w_ready = sem("w_ready")
        gm_done = sem("gm_done")
        g_ready = sem("g_ready")
        m_hi_ready = sem("m_hi_ready")
        m_ready = sem("m_ready")
        q_done = sem("q_done")
        q_hi_ready = sem("q_hi_ready")
        q_ready = sem("q_ready")
        lat_done = sem("lat_done")
        swap_half = sem("swap_half")
        swap_ready = sem("swap_ready")
        sine_ready = sem("sine_ready")
        cosine_ready = sem("cosine_ready")
        rope_ready = sem("rope_ready")
        u_done = sem("u_done")
        u_hi_ready = sem("u_hi_ready")
        u_ready = sem("u_ready")
        sc_done = sem("sc_done")
        max_ready = sem("max_ready")
        exp_ready = sem("exp_ready")
        inv_ready = sem("inv_ready")
        prob_ready = sem("prob_ready")
        pT_done = sem("pT_done")
        pT_hi_ready = sem("pT_hi_ready")
        pT_ready = sem("pT_ready")
        cx_done = sem("cx_done")
        cx_hi_ready = sem("cx_hi_ready")
        cx_ready = sem("cx_ready")
        o_done = sem("o_done")
        acc_ready = sem("acc_ready")

        def latent_bank(c, i):
            return (bank_b + bank_q + bank_b[0:1])[QC * c + i]

        def score_bank(b, hh):
            return bank_b[(HQ * b + hh + 1) % 3]

        ROPE = [(0, 1, 2), (3, 4, 5, 6, 7)]
        KV_ORDER = (3, 4, 5, 6, 0, 1, 2, 7)

        def rope_context(engine, kind):
            half = DC // 2
            for n, b in enumerate(ROPE[kind]):
                at = slice(LC * b, LC * (b + 1))
                engine.tensor_tensor(kv_rot[:, at, 0:half], kv_raw[:, at, half:DC], sin_k[:, :, 0:half], ALU.mult).then_inc(rope_step[kind], 1)
                engine.tensor_tensor(kv_rot[:, at, half:DC], kv_raw[:, at, 0:half], sin_k[:, :, half:DC], ALU.mult).then_inc(rope_step[kind], 1)
                engine.tensor_tensor(kvr[:, at, :], kv_raw[:, at, :], cos_k[:], ALU.mult).then_inc(rope_step[kind], 1)
                engine.wait_ge(rope_step[kind], 3 * n + 3)
                engine.tensor_tensor(kvr[:, at, :], kvr[:, at, :], kv_rot[:, at, :], ALU.add).then_inc(kvr_ready[kind], 1)

        def wait_roped(engine, b):
            kind = 0 if b in ROPE[0] else 1
            engine.wait_ge(kvr_ready[kind], ROPE[kind].index(b) + 1)

        block = ctx.enter_context(nc.Block())

        HEAD_DMAS = 6 * 16

        @block.sync
        def _(sp):
            def load_head(h, s):
                for dst, name in ((wq_raw, "wq"), (wc_raw, "wc"), (wqr, "wqr"), (wkr, "wkr"), (wkv, "wkv"), (wo, "wo")):
                    sp.dma_start(dst[:, s], io[name][h]).then_inc(head_loaded[s], 16)

            for c in range(4):
                sp.dma_start(acc[:, 2 * c:2 * c + 2, :], io["x"].rearrange("(b s) d -> s b d", s=S)[:, 2 * c:2 * c + 2, :]).then_inc(x_loaded[c], 16)
            sp.dma_start(gate_col[:], io["g_xattn"].partition_broadcast(P)).then_inc(gate_loaded, 16)
            sp.dma_start(ffn_gate[:], io["g_ffn"].partition_broadcast(P)).then_inc(gate_loaded, 16)
            sp.dma_start(cos_k[:], io["cos_k"]).then_inc(kv_loaded, 16)
            sp.dma_start(sin_k[:], io["sin_k"]).then_inc(kv_loaded, 16)
            sp.dma_start(kv_raw[:].rearrange("p (b c) d -> p b c d", c=LC),
                         io["ctx"].rearrange("b (c p) d -> p b c d", p=LP)).then_inc(kv_loaded, 16)
            sp.dma_start(ident[:], io["ident"]).then_inc(ident_loaded, 16)
            load_head(0, 0)
            sp.dma_start(cos_q[:], io["cos_q"]).then_inc(const_loaded, 16)
            sp.dma_start(sin_q[:], io["sin_q"]).then_inc(const_loaded, 16)
            load_head(1, 1)
            with sp.Fori(0, H // 2 - 1) as i:
                for s in range(2):
                    sp.wait_ge(w_ready, 2 * (2 * i + s) + 2)
                    sp.sem_inc(w_slot_free, 1)
                    sp.wait_ge(gm_done, 2 * i + s + 1)
                    load_head(2 * i + s + 2, s)

        @block.gpsimd
        def _(pool):
            pool.memset(kvT_hi[:, :, L:LE].bitcast(F32), 0.0).then_inc(pad_ready, 1)
            pool.memset(kvT_lo[:, :, L:LE].bitcast(F32), 0.0).then_inc(pad_ready, 1)

            def low_part(h, s):
                pool.wait_ge(w_hi_ready, 2 * h + 1)
                pool.tensor_tensor(wq_lo[:, s], wq_raw[:, s], wq_hi[:, s].bitcast(F32), ALU.subtract).then_inc(w_ready, 1)
                pool.wait_ge(w_hi_ready, 2 * h + 2)
                pool.tensor_tensor(wc_lo[:, s], wc_raw[:, s], wc_hi[:, s].bitcast(F32), ALU.subtract).then_inc(w_ready, 1)

            pool.wait_ge(kv_loaded, 48)
            rope_context(nc.gpsimd, 1)
            pool.wait_ge(const_loaded, 32)
            with pool.Fori(0, NQ) as j:
                low_part(HQ * j, 0)
                low_part(HQ * j + 1, 1)
                for k in range(HQ):
                    for c in range(2):
                        for i in range(QC):
                            pool.wait_ge(swap_ready, QC * (2 * (HQ * j + k) + c) + i + 1)
                            v = turned[:, c, i, :].rearrange("p (b s) -> p b s", s=S)
                            pool.tensor_tensor(v, v, sin_q[:, i:i + 1, :].to_broadcast([P, B // 2, S]), ALU.mult).then_inc(sine_ready, 1)
                    if k + 2 < HQ:
                        low_part(HQ * j + k + 2, k % 2)
                for b in range(B):
                    for hh in range(HQ):
                        pool.wait_ge(inv_ready, HQ * (B * j + b) + hh + 1)
                        pool.tensor_tensor(probs[:, hh, :], probs[:, hh, :], rinv[:, hh:hh + 1].to_broadcast([S, L]), ALU.mult).then_inc(prob_ready, 1)

        @block.scalar
        def _(act):
            act.wait_ge(gate_loaded, 32)
            nc.scalar.activation(ffn_gate[:], ffn_gate[:], ACT.Tanh)
            nc.scalar.activation(tanh_gate[:], gate_col[:], ACT.Tanh).then_inc(tanh_ready, 1)
            act.wait_ge(eps_ready, 1)
            act.wait_ge(mv_ready, B)
            nc.scalar.activation(rstd[:], mean_var[:, :, 1], ACT.Sqrt, bias=eps_col[0:S]).then_inc(std_ready, 1)
            for n in range(B):
                act.wait_ge(setup_T, n + 1)
                nc.scalar.activation(xnT_hi[:, :, n * S:(n + 1) * S], bank_b[n % 3][:, 0:DK * S].rearrange("p (k s) -> p k s", k=DK),
                                     ACT.Copy).then_inc(setup_hi, 1)
            for n, b in enumerate(KV_ORDER, B):
                at = slice(LC * b, LC * (b + 1))
                wait_roped(act, b)
                nc.scalar.activation(kvr_hi[:, at, :], kvr[:, at, :], ACT.Copy).then_inc(kvr_hi_ready, 1)
                act.wait_ge(setup_T, n + 1)
                nc.scalar.activation(kvT_hi[:, b, 0:L], bank_b[n % 3][:, 0:L], ACT.Copy).then_inc(setup_hi, 1)

            with act.Fori(0, NQ) as j:
                def g_and_m(k):
                    h = HQ * j + k
                    act.wait_ge(gm_done, h + 1)
                    if k >= 2:
                        act.wait_ge(u_done, 2 * (h - 2) + 2)
                    nc.scalar.activation(g_mat[:, k % 2, :, :], bank_g[0][:, 0:QC * DC].rearrange("p (c d) -> p c d", c=QC),
                                         ACT.Copy).then_inc(g_ready, 1)
                    nc.scalar.activation(m_hi[:, k, :], bank_m[:, :], ACT.Copy, scale=tanh_gate[:]).then_inc(m_hi_ready, 1)

                def q_high(k):
                    for c in range(2):
                        act.wait_ge(q_done, 2 * (HQ * j + k) + c + 1)
                        nc.scalar.activation(qhk_hi[:, c, :], bank_q[c][:, 0:TC], ACT.Copy).then_inc(q_hi_ready, 1)

                def u_high(k, c):
                    act.wait_ge(u_done, 2 * (HQ * j + k) + c + 1)
                    nc.scalar.activation(u_hi[:, k, c * TC:(c + 1) * TC], bank_g[1 - c][:, 0:TC], ACT.Copy).then_inc(u_hi_ready, 1)

                def exp(b, hh):
                    n = HQ * (B * j + b) + hh
                    act.wait_ge(max_ready, n + 1)
                    if b:
                        act.wait_ge(pT_done, n - HQ + 1)
                    nc.scalar.activation(probs[:, hh, :], score_bank(b, hh)[0:S, 0:L], ACT.Exp, bias=nmax[:, hh:hh + 1],
                                         accum_out=rowsum[:, hh:hh + 1]).then_inc(exp_ready, 1)

                def w_high(k):
                    t = k % 2
                    act.wait_ge(head_loaded[t], HEAD_DMAS * (2 * j + k // 2 + 1))
                    if k >= 2:
                        act.wait_ge(lat_done, 2 * QC * (HQ * j + k - 1))
                    nc.scalar.activation(wq_hi[:, t], wq_raw[:, t], ACT.Copy).then_inc(w_hi_ready, 1)
                    nc.scalar.activation(wc_hi[:, t], wc_raw[:, t], ACT.Copy).then_inc(w_hi_ready, 1)

                w_high(0)
                act.wait_ge(tanh_ready, 1)
                g_and_m(0)
                w_high(1)
                q_high(0)
                for k in range(HQ):
                    h = HQ * j + k
                    half = P // 2
                    for c in range(2):
                        for i in range(QC):
                            n = QC * (2 * h + c) + i
                            act.wait_ge(lat_done, n + 1)
                            if k:
                                act.wait_ge(rope_ready, n - 2 * QC + 1)
                            lat = latent_bank(c, i)
                            nc.scalar.activation(turned[0:half, c, i, :], lat[half:P, 0:TC], ACT.Copy).then_inc(swap_half, 1)
                            nc.scalar.activation(turned[half:P, c, i, :], lat[0:half, 0:TC], ACT.Copy).then_inc(swap_ready, 1)
                    if k + 1 < HQ:
                        g_and_m(k + 1)
                        q_high(k + 1)
                        if k + 2 < HQ:
                            w_high(k + 2)
                        for c in range(2):
                            u_high(k, c)
                exp(0, 0)
                exp(0, 1)
                u_high(HQ - 1, 0)
                u_high(HQ - 1, 1)
                exp(0, 2)
                exp(0, 3)

                def context_hi(b):
                    g = B * j + b
                    act.wait_ge(cx_done, g + 1)
                    if b >= 2:
                        act.wait_ge(o_done, g - 1)
                    nc.scalar.activation(cx_hi[:, b % 2, :], bank_m[:, 0:HQ * S], ACT.Copy).then_inc(cx_hi_ready, 1)

                for b in range(B):
                    g = B * j + b
                    for hh in range(HQ):
                        n = HQ * g + hh
                        act.wait_ge(pT_done, n + 1)
                        if b >= 2 and hh == 0:
                            act.wait_ge(cx_done, g - 1)
                        nc.scalar.activation(pT_hi[:, b % 2, :, hh * S:(hh + 1) * S],
                                             bank_g[hh % 2][0:LP, 0:LC * S].rearrange("p (c s) -> p c s", c=LC), ACT.Copy).then_inc(pT_hi_ready, 1)
                        if b + 1 < B:
                            exp(b + 1, hh)
                    if b:
                        context_hi(b - 1)
                context_hi(B - 1)

        @block.vector
        def _(dve):
            dve.sem_inc(acc_ready, 1)
            nc.vector.memset(eps_col[:], EPS).then_inc(eps_ready, 1)
            for b in range(B):
                dve.wait_ge(x_loaded[b // 2], 16)
                nc.vector.bn_stats(stats[:, b, :], acc[:, b, :]).then_inc(stats_ready, 1)
            for b in range(B):
                dve.wait_ge(stats_ready, b + 1)
                nc.vector.bn_aggr(mean_var[:, b, :], stats[:, b, :]).then_inc(mv_ready, 1)
            dve.wait_ge(std_ready, 1)
            nc.vector.reciprocal(rstd[:], rstd[:]).then_inc(rstd_ready, 1)
            dve.wait_ge(rstd_ready, 1)
            for b in range(B):
                nc.vector.tensor_scalar(xn[:, b, :], acc[:, b, :], mean_var[:, b, 0:1], rstd[:, b:b + 1],
                                        ALU.subtract, ALU.mult).then_inc(xn_ready, 1)
            for n in range(B):
                dve.wait_ge(setup_hi, n + 1)
                nc.vector.tensor_tensor(xnT_lo[:, :, n * S:(n + 1) * S], bank_b[n % 3][:, 0:DK * S].rearrange("p (k s) -> p k s", k=DK),
                                        xnT_hi[:, :, n * S:(n + 1) * S].bitcast(F32), ALU.subtract).then_inc(setup_lo, 1)
            dve.wait_ge(kv_loaded, 48)
            rope_context(nc.vector, 0)
            for n, b in enumerate(KV_ORDER, B):
                dve.wait_ge(setup_hi, n + 1)
                nc.vector.tensor_tensor(kvT_lo[:, b, 0:L], bank_b[n % 3][:, 0:L], kvT_hi[:, b, 0:L].bitcast(F32),
                                        ALU.subtract).then_inc(setup_lo, 1)
            dve.wait_ge(kvr_hi_ready, B)
            for kind in range(2):
                dve.wait_ge(kvr_ready[kind], len(ROPE[kind]))
            nc.vector.tensor_tensor(kvr_lo[:], kvr[:], kvr_hi[:].bitcast(F32), ALU.subtract).then_inc(kvr_lo_ready, 1)
            dve.wait_ge(const_loaded, 32)
            dve.wait_ge(tanh_ready, 1)

            with dve.Fori(0, NQ) as j:
                def m_low(k):
                    dve.wait_ge(m_hi_ready, HQ * j + k + 1)
                    nc.vector.scalar_tensor_tensor(out=m_lo[:, k, :], in0=bank_m[:, :], scalar=tanh_gate[:], in1=m_hi[:, k, :].bitcast(F32),
                                                   op0=ALU.mult, op1=ALU.subtract).then_inc(m_ready, 1)

                def q_low(k):
                    for c in range(2):
                        dve.wait_ge(q_hi_ready, 2 * (HQ * j + k) + c + 1)
                        nc.vector.tensor_tensor(qhk_lo[:, c, :], bank_q[c][:, 0:TC], qhk_hi[:, c, :].bitcast(F32), ALU.subtract).then_inc(q_ready, 1)

                def cosine_part(k, c, i):
                    n = QC * (2 * (HQ * j + k) + c) + i
                    dve.wait_ge(swap_ready, n + 1)
                    nc.vector.tensor_tensor(roped[:, c, i, :].rearrange("p (b s) -> p b s", s=S),
                                            latent_bank(c, i)[:, 0:TC].rearrange("p (b s) -> p b s", s=S),
                                            cos_q[:, i:i + 1, :].to_broadcast([P, B // 2, S]), ALU.mult).then_inc(cosine_ready, 1)

                def add_sine(k, c, i):
                    n = QC * (2 * (HQ * j + k) + c) + i
                    dve.wait_ge(cosine_ready, n + 1)
                    dve.wait_ge(sine_ready, n + 1)
                    nc.vector.tensor_tensor(roped[:, c, i, :], roped[:, c, i, :], turned[:, c, i, :], ALU.add).then_inc(rope_ready, 1)

                def u_low(k, c):
                    dve.wait_ge(u_hi_ready, 2 * (HQ * j + k) + c + 1)
                    nc.vector.tensor_tensor(u_lo[:, k, c * TC:(c + 1) * TC], bank_g[1 - c][:, 0:TC], u_hi[:, k, c * TC:(c + 1) * TC].bitcast(F32),
                                            ALU.subtract).then_inc(u_ready, 1)

                def row_max(b, hh):
                    n = HQ * (B * j + b) + hh
                    dve.wait_ge(sc_done, n + 1)
                    nc.vector.tensor_reduce(nmax[:, hh:hh + 1], score_bank(b, hh)[0:S, 0:L], AX_X, ALU.max,
                                            negate=True).then_inc(max_ready, 1)

                def invert_sum(b, hh):
                    n = HQ * (B * j + b) + hh
                    dve.wait_ge(exp_ready, n + 1)
                    nc.vector.reciprocal(rinv[:, hh:hh + 1], rowsum[:, hh:hh + 1]).then_inc(inv_ready, 1)

                def accumulate(b):
                    g = B * j + b
                    dve.wait_ge(o_done, g + 1)
                    nc.vector.tensor_tensor(acc[:, b, :], bank_q[b % 2][0:S, :], acc[:, b, :], ALU.add).then_inc(acc_ready, 1)

                def context_lo(b):
                    dve.wait_ge(cx_hi_ready, B * j + b + 1)
                    nc.vector.tensor_tensor(cx_lo[:, b % 2, :], bank_m[:, 0:HQ * S], cx_hi[:, b % 2, :].bitcast(F32),
                                            ALU.subtract).then_inc(cx_ready, 1)

                m_low(0)
                q_low(0)
                for k in range(HQ):
                    for i in range(QC):
                        cosine_part(k, 0, i)
                    for i in range(QC):
                        cosine_part(k, 1, i)
                        add_sine(k, 0, i)
                    if k + 1 == HQ:
                        row_max(0, 0)
                        row_max(0, 1)
                    for i in range(QC):
                        add_sine(k, 1, i)
                    if k + 1 < HQ:
                        m_low(k + 1)
                        q_low(k + 1)
                        for c in range(2):
                            u_low(k, c)
                invert_sum(0, 0)
                invert_sum(0, 1)
                u_low(HQ - 1, 0)
                u_low(HQ - 1, 1)
                row_max(0, 2)
                row_max(0, 3)
                invert_sum(0, 2)
                invert_sum(0, 3)
                for b in range(B):
                    g = B * j + b
                    for hh in range(HQ):
                        n = HQ * g + hh
                        if b + 1 < B:
                            row_max(b + 1, hh)
                        dve.wait_ge(pT_hi_ready, n + 1)
                        nc.vector.tensor_tensor(pT_lo[:, b % 2, :, hh * S:(hh + 1) * S],
                                                bank_g[hh % 2][0:LP, 0:LC * S].rearrange("p (c s) -> p c s", c=LC),
                                                pT_hi[:, b % 2, :, hh * S:(hh + 1) * S].bitcast(F32), ALU.subtract).then_inc(pT_ready, 1)
                        if b + 1 < B:
                            invert_sum(b + 1, hh)
                        if b >= 3 and hh == 0:
                            accumulate(b - 3)
                    if b:
                        context_lo(b - 1)
                accumulate(B - 3)
                context_lo(B - 1)
                accumulate(B - 2)
                accumulate(B - 1)

        @block.tensor
        def _(pe):
            mm = nc.tensor.matmul
            pe.wait_ge(ident_loaded, 16)
            for n in range(B):
                pe.wait_ge(xn_ready, n + 1)
                if n >= 3:
                    pe.wait_ge(setup_lo, n - 2)
                for k in range(DK):
                    last = nc.tensor.transpose(bank_b[n % 3][:, k * S:(k + 1) * S], xn[:, n, k * P:(k + 1) * P], ident[0:S, 0:S])
                last.then_inc(setup_T, 1)
            for n, b in enumerate(KV_ORDER, B):
                wait_roped(pe, b)
                pe.wait_ge(setup_lo, n - 2)
                for c in range(LC):
                    last = nc.tensor.transpose(bank_b[n % 3][:, c * LP:(c + 1) * LP], kvr[:, LC * b + c, :], ident[0:LP, 0:LP])
                last.then_inc(setup_T, 1)
            pe.wait_ge(setup_lo, 2 * B)
            pe.wait_ge(pad_ready, 2)

            with pe.Fori(0, NQ) as j:
                def g_and_m(k):
                    h = HQ * j + k
                    s = k % 2
                    pe.wait_ge(head_loaded[s], HEAD_DMAS * (2 * j + k // 2 + 1))
                    if k == 1:
                        pe.wait_ge(g_ready, h)
                    elif k:
                        pe.wait_ge(u_ready, 2 * (h - 1))
                    for c in range(QC):
                        mm(bank_g[0][:, c * DC:(c + 1) * DC], wqr[:, s, c * P:(c + 1) * P], wkr[:, s, :], start=True, stop=True)
                    if k:
                        pe.wait_ge(m_ready, h)
                    mm(bank_m[:, :], wkv[:, s, :], wo[:, s, :], start=True, stop=True).then_inc(gm_done, 1)

                def q_head(k):
                    s = k % 2
                    pe.wait_ge(w_ready, 2 * (HQ * j + k) + 1)
                    for c in range(2):
                        if k == 0 and c == 0:
                            pe.wait_ge(acc_ready, B * j + 1)
                        if k:
                            pe.wait_ge(cosine_ready, 2 * QC * (HQ * j + k - 1) + QC + c + 1)
                        at = slice(c * TC, (c + 1) * TC)
                        for i in range(DK):
                            last = three_pass(mm, bank_q[c][:, 0:TC], wq_hi[:, s, i, :], wq_lo[:, s, i, :], xnT_hi[:, i, at], xnT_lo[:, i, at],
                                              i == 0, i == DK - 1)
                        last.then_inc(q_done, 1)

                def latents(k, c):
                    m = 2 * (HQ * j + k) + c
                    pe.wait_ge(q_ready, m + 1)
                    pe.wait_ge(w_ready, 2 * (HQ * j + k) + 2)
                    for i in range(QC):
                        if c and i == QC - 1:
                            pe.wait_ge(cosine_ready, QC * (m - 1) + 1)
                        at = slice(i * P, (i + 1) * P)
                        three_pass(mm, latent_bank(c, i)[:, 0:TC], wc_hi[:, k % 2, at], wc_lo[:, k % 2, at],
                                   qhk_hi[:, c, :], qhk_lo[:, c, :], True, True).then_inc(lat_done, 1)

                def score_query(k, c):
                    h = HQ * j + k
                    m = 2 * h + c
                    if c == 0:
                        pe.wait_ge(g_ready, h + 1)
                        if k:
                            pe.wait_ge(u_ready, m - 1)
                    elif k + 1 < HQ:
                        pe.wait_ge(g_ready, h + 2)
                    else:
                        pe.wait_ge(u_ready, m - 1)
                    for i in range(QC):
                        pe.wait_ge(rope_ready, QC * m + i + 1)
                        last = mm(bank_g[1 - c][:, 0:TC], g_mat[:, k % 2, i, :], roped[:, c, i, :], start=(i == 0), stop=(i == QC - 1))
                    last.then_inc(u_done, 1)

                def scores(b, hh):
                    n = HQ * (B * j + b) + hh
                    if HQ * b + hh >= 3:
                        pe.wait_ge(exp_ready, n - 2)
                    at = slice(b * S, (b + 1) * S)
                    three_pass(mm, score_bank(b, hh)[0:S, 0:LE], u_hi[:, hh, at], u_lo[:, hh, at], kvT_hi[:, b, :], kvT_lo[:, b, :],
                               True, True).then_inc(sc_done, 1)

                g_and_m(0)
                q_head(0)
                for k in range(HQ):
                    for c in range(2):
                        latents(k, c)
                    if k + 1 < HQ:
                        g_and_m(k + 1)
                        q_head(k + 1)
                        for c in range(2):
                            score_query(k, c)
                last_h = HQ * j + HQ - 1
                pe.wait_ge(cosine_ready, 2 * QC * last_h + 2)
                scores(0, 0)
                pe.wait_ge(cosine_ready, 2 * QC * last_h + 3)
                scores(0, 1)
                score_query(HQ - 1, 0)
                score_query(HQ - 1, 1)
                scores(0, 2)
                pe.wait_ge(u_ready, 2 * last_h + 1)
                scores(0, 3)

                def turn(b, hh):
                    n = HQ * (B * j + b) + hh
                    pe.wait_ge(prob_ready, n + 1)
                    if HQ * b + hh >= 2:
                        pe.wait_ge(pT_ready, n - 1)
                    for c in range(LC):
                        last = nc.tensor.transpose(bank_g[hh % 2][0:LP, c * S:(c + 1) * S], probs[:, hh, c * LP:(c + 1) * LP], ident[0:S, 0:S])
                    last.then_inc(pT_done, 1)

                def attend(b, c):
                    g = B * j + b
                    if c == 0:
                        pe.wait_ge(pT_ready, HQ * g + HQ)
                        if b:
                            pe.wait_ge(cx_ready, g)
                    last = three_pass(mm, bank_m[:, 0:HQ * S], kvr_hi[:, LC * b + c, :], kvr_lo[:, LC * b + c, :],
                                      pT_hi[:, b % 2, c, :], pT_lo[:, b % 2, c, :], c == 0, c == LC - 1)
                    if c == LC - 1:
                        last.then_inc(cx_done, 1)

                def project(b, hh):
                    g = B * j + b
                    if hh == 0:
                        pe.wait_ge(cx_ready, g + 1)
                        if b >= 2:
                            pe.wait_ge(acc_ready, g)
                    at = slice(hh * S, (hh + 1) * S)
                    last = three_pass(mm, bank_q[b % 2][0:S, :], cx_hi[:, b % 2, at], cx_lo[:, b % 2, at], m_hi[:, hh, :], m_lo[:, hh, :],
                                      hh == 0, hh == HQ - 1)
                    if hh == HQ - 1:
                        last.then_inc(o_done, 1)

                pe.wait_ge(u_ready, 2 * HQ * j + 2 * HQ)
                pe.wait_ge(m_ready, HQ * j + HQ)
                pe.wait_ge(kvr_lo_ready, 1)
                for b in range(B):
                    for hh in range(HQ):
                        turn(b, hh)
                        if b + 1 < B:
                            scores(b + 1, hh)
                        if b and hh:
                            attend(b - 1, hh - 1)
                        if b >= 2 and hh:
                            project(b - 2, hh - 1)
                    if b >= 2:
                        project(b - 2, HQ - 1)
                for hh in range(HQ):
                    project(B - 2, hh)
                    if hh < LC:
                        attend(B - 1, hh)
                for hh in range(HQ):
                    project(B - 1, hh)


E = 8
TOPK = 4
FI = 1024
FK = FI // P
CAP = 512
BLK = CAP // P
MAXOVF = TOPK * B * S // (CAP + 1)
NI = E + MAXOVF
NIT = 16
UNIT = 1024
NU = 16
RAW = 4
HOT = 3
AHEAD = 4
RING = 8
ROWS = B * S + CAP


def build_experts(nc, io, out, keep):
    acc, ident, ffn_gate = keep["acc"], keep["ident"], keep["ffn_gate"]
    assert B * S <= 2 * CAP
    with ExitStack() as ctx:
        def sb(name, shape, dt=F32):
            return ctx.enter_context(nc.sbuf_tensor(name, shape, dt))

        def sem(name):
            return ctx.enter_context(nc.semaphore(name))

        def psum(name, shape):
            return ctx.enter_context(nc.psum_tensor(name, shape, F32))

        xn_rows = nc.dram_tensor("xn_rows", [ROWS, D], F32, kind="Internal").ap()
        sum_rows = out

        bank_h = [psum(f"bank_h{i}", [P, 512]) for i in range(3)]
        bank_y = [psum(f"bank_y{i}", [P, 512]) for i in range(BLK)]
        bank_t = psum("bank_t", [P, 512])

        raw = sb("raw", [P, RAW, UNIT])
        w_hi = sb("w_hi", [P, RING, UNIT], F32R)
        w_lo = sb("w_lo", [P, RING, UNIT], F32R)
        iota = sb("iota", [S, CAP])
        pad_row = sb("pad_row", [P, BLK])
        pos_tab = sb("pos_tab", [S, NIT, B])
        row_tab = sb("row_tab", [S, NIT, B, 4], F32R)
        experts = sb("experts", [1, NIT], mybir.dt.int32)
        n_items = sb("n_items", [1, 1], mybir.dt.int32)
        idx_next = sb("idx_next", [P, BLK], U32)
        idx = sb("idx", [P, BLK], U32)
        gate_next = sb("gate_next", [P, BLK])
        gate = sb("gate", [P, BLK])
        lists = sb("lists", [P, BLK, 4])
        row_f = sb("row_f", [P, BLK])

        routing = ExitStack()

        def rb(name, shape, dt=F32):
            return routing.enter_context(nc.sbuf_tensor(name, shape, dt))

        xn2 = rb("xn2", [S, B, D])
        xn2T = rb("xn2T", [P, DK, B * S])
        router = rb("router", [P, DK, E])
        stats = rb("stats2", [S, B, 6])
        mean_var = rb("mean_var2", [S, B, 2])
        rstd = rb("rstd2", [S, B])
        eps_col = rb("eps_col2", [P, 1])
        before = rb("before", [S, E, E])
        upper = rb("upper", [S, S])
        upper_r = rb("upper_r", [S, S], F32R)
        ones = rb("ones", [S, P])
        ones_r = rb("ones_r", [S, P], F32R)
        token_row = rb("token_row", [S, B])
        expert_id = rb("expert_id", [P, E])
        zeros = rb("zeros", [P, D])
        logits = rb("logits", [S, B, E])
        pair = rb("pair", [S, B, E, E])
        pair2 = rb("pair2", [S, B, E, E])
        rank = rb("rank", [S, B, E])
        mask = rb("mask", [S, B, E])
        mask_r = rb("mask_r", [S, B, E], F32R)
        lmax = rb("lmax", [S, B])
        prob = rb("prob", [S, B, E])
        psum_k = rb("psum_k", [S, B])
        gates = rb("gates", [S, B, E])
        posm = rb("posm", [S, B, E])
        count = rb("count", [P, E])
        ovf = rb("ovf", [P, E])
        ovf_pair = rb("ovf_pair", [P, E, E])
        ovf_at = rb("ovf_at", [P, E])
        n_ovf = rb("n_ovf", [P, 1])
        sel = rb("sel", [P, E, E])
        items_f = rb("items_f", [P, NIT])
        gate_ovf = rb("gate_ovf", [S, E, B])
        routing.close()

        onehot = sb("onehot", [S, HOT, CAP], F32R)
        xg = sb("xg", [P, BLK, D])
        xT_hi = sb("xT_hi", [P, DK, CAP], F32R)
        xT_lo = sb("xT_lo", [P, DK, CAP], F32R)
        h_full = sb("h_full", [P, 2, CAP])
        h_hi = [sb(f"h{i}_hi", [P, FK, CAP], F32R) for i in (1, 2)]
        h_lo = [sb(f"h{i}_lo", [P, FK, CAP], F32R) for i in (1, 2)]
        y_sb = sb("y_sb", [P, BLK, D])

        route_loaded = sem("route_loaded")
        rows_stored = sem("rows_stored")
        zeros_ready = sem("zeros_ready")
        eps2_ready = sem("eps2_ready")
        route_step = sem("route_step")
        mv2_ready = sem("mv2_ready")
        std2_ready = sem("std2_ready")
        xn2_ready = sem("xn2_ready")
        xn2T_done = sem("xn2T_done")
        xn2T_ready = sem("xn2T_ready")
        logits_done = sem("logits_done")
        shifted_ready = sem("shifted_ready")
        exp2_ready = sem("exp2_ready")
        mask_ready = sem("mask_ready")
        pos_done = sem("pos_done")
        tables_ready = sem("tables_ready")

        raw_loaded = [sem(f"raw_loaded{i}") for i in range(RAW)]
        unit_hi = sem("unit_hi")
        unit_lo = sem("unit_lo")
        unit_used = sem("unit_used")
        hot_ready = sem("hot_ready")
        hot_used = sem("hot_used")
        list_step = sem("list_step")
        idx_ready = sem("idx_ready")
        gather_begins = sem("gather_begins")
        scatter_begins = sem("scatter_begins")
        load_begins = sem("load_begins")
        gathered = [sem(f"gathered{i}") for i in range(BLK)]
        xT_done = sem("xT_done")
        xT_hi_ready = sem("xT_hi_ready")
        xT_ready = sem("xT_ready")
        h_done = sem("h_done")
        h_hi_ready = sem("h_hi_ready")
        h_ready = sem("h_ready")
        y_done = sem("y_done")
        cur_ready = sem("cur_ready")
        y_ready = sem("y_ready")
        scattered = sem("scattered")
        y_free = sem("y_free")

        def turn_bank(n, i):
            return bank_y[i] if isinstance(n, int) else bank_t

        block = ctx.enter_context(nc.Block())

        TURN_H = (14, 15)
        TURN_W = (12, 13)
        LAG = 2

        def unit_of(m):
            return m // 2 if m < FK else m - FK + 4

        def items_count(eng):
            eng.wait_ge(tables_ready, 2)
            return eng.value_load(n_items[0:1, 0:1], min_val=E, max_val=NI)

        @block.sync
        def _(sp):
            def load(e, u):
                sp.dma_start(raw[:, u % RAW, :], io["units"][bass.ds(e, 1), u].rearrange("e p n -> (e p) n")).then_inc(raw_loaded[u % RAW], 16)

            for dst, name in ((router, "router"), (before, "before"), (upper, "upper"), (ones, "ones"), (token_row, "token_row"),
                              (expert_id, "expert_id"), (pad_row, "pad_row")):
                sp.dma_start(dst[:], io[name]).then_inc(route_loaded, 16)
            sp.dma_start(iota[:], io["iota"].partition_broadcast(S)).then_inc(route_loaded, 16)
            for u in range(AHEAD):
                load(0, u)
            sp.dma_start(sum_rows[0:B * S, :].rearrange("(b s) d -> s b d", s=S), acc[:]).then_inc(rows_stored, 16)
            sp.wait_ge(zeros_ready, 1)
            for rows in (xn_rows, sum_rows):
                sp.dma_start(rows[B * S:ROWS, :].rearrange("(i p) d -> p i d", p=P), zeros[:].unsqueeze(1).to_broadcast([P, BLK, D])).then_inc(rows_stored, 16)
            sp.wait_ge(xn2_ready, B)
            sp.dma_start(xn_rows[0:B * S, :].rearrange("(b s) d -> s b d", s=S), xn2[:]).then_inc(rows_stored, 16)
            items = items_count(sp)
            with sp.Fori(0, items) as w:
                e = sp.value_load(experts[0:1, bass.ds(w, 1)], min_val=0, max_val=E - 1)
                for u in range(NU - AHEAD):
                    sp.wait_ge(unit_lo, NU * w + u + 1)
                    sp.sem_inc(load_begins, 1)
                    load(e, u + AHEAD)
                e = sp.value_load(experts[0:1, bass.ds(w + 1, 1)], min_val=0, max_val=E - 1)
                for u in range(NU - AHEAD, NU):
                    sp.wait_ge(unit_lo, NU * w + u + 1)
                    sp.sem_inc(load_begins, 1)
                    load(e, u + AHEAD - NU)
            sp.wait_ge(rows_stored, 64)
            sp.wait_ge(y_free, items + 1)
            sp.sem_inc(load_begins, 1)

        @block.gpsimd
        def _(pool):
            pool.memset(zeros[:], 0.0).then_inc(zeros_ready, 1)
            pool.sem_inc(y_free, 1)
            for u in range(AHEAD):
                pool.wait_ge(unit_hi, u + 1)
                pool.tensor_tensor(w_lo[:, u, :], raw[:, u, :], w_hi[:, u, :].bitcast(F32), ALU.subtract).then_inc(unit_lo, 1)
            pool.wait_ge(rows_stored, 64)

            def gather(n):
                pool.wait_ge(idx_ready, n + 1)
                pool.sem_inc(gather_begins, 1)
                for i in range(BLK):
                    pool.indirect_dma_start(xg[:, i, :], None, xn_rows, bass.IndirectOffsetOnAxis(ap=idx_next[:, i:i + 1], axis=0)).then_inc(gathered[i], 16)

            gather(0)
            items = items_count(pool)
            with pool.Fori(0, items) as w:
                gather(w + 1)
                pool.wait_ge(y_ready, BLK * w + BLK)
                pool.sem_inc(scatter_begins, 1)
                for i in range(BLK):
                    pool.indirect_dma_start(sum_rows, bass.IndirectOffsetOnAxis(ap=idx[:, i:i + 1], axis=0), y_sb[:, i, :], None,
                                            compute_op=ALU.add).then_inc(scattered, 16)
                pool.wait_ge(scattered, 16 * BLK * (w + 1))
                pool.sem_inc(y_free, 1)

        @block.scalar
        def _(act):
            act.wait_ge(eps2_ready, 1)
            for half in (slice(0, B // 2), slice(B // 2, B)):
                act.wait_ge(mv2_ready, half.stop)
                nc.scalar.activation(rstd[:, half], mean_var[:, half, 1], ACT.Sqrt, bias=eps_col[0:S]).then_inc(std2_ready, 1)

            def unit(w, u):
                act.wait_ge(raw_loaded[u % RAW], 16 * ((NU // RAW) * w + u // RAW + 1))
                if AHEAD <= u < RING - 1:
                    act.wait_ge(unit_used, (AHEAD - 1) * w + u - AHEAD + 1)
                elif u == RING - 1:
                    act.wait_ge(y_done, BLK * w + BLK)
                elif RING <= u < RING + 4:
                    act.wait_ge(h_done, 2 * FK * w + 2 * (u - RING) + 2)
                elif u >= RING + 4:
                    act.wait_ge(h_done, 2 * FK * w + FK + u - RING - 4 + 1)
                nc.scalar.activation(w_hi[:, u % RING, :], raw[:, u % RAW, :], ACT.Copy).then_inc(unit_hi, 1)

            def turned(n, i):
                act.wait_ge(xT_done, BLK * n + i + 1)
                nc.scalar.activation(xT_hi[:, :, i * P:(i + 1) * P], turn_bank(n, i)[:, :].rearrange("p (k s) -> p k s", k=DK), ACT.Copy).then_inc(xT_hi_ready, 1)

            for b in range(B):
                act.wait_ge(xn2T_done, b + 1)
                nc.scalar.activation(xn2T[:, :, b * S:(b + 1) * S], bank_h[b % 3][:, 0:DK * S].rearrange("p (k s) -> p k s", k=DK),
                                     ACT.Copy).then_inc(xn2T_ready, 1)
                if b % 2:
                    unit(0, b // 2)
            act.wait_ge(shifted_ready, 1)
            nc.scalar.activation(prob[:], prob[:], ACT.Exp).then_inc(exp2_ready, 1)
            for i in range(BLK):
                turned(0, i)
            items = items_count(act)
            with act.Fori(0, items) as w:
                for m in range(2 * FK):
                    n = 2 * FK * w + m
                    act.wait_ge(h_done, n + 1)
                    if m >= 2:
                        act.wait_ge(h_ready, n - 1)
                    nc.scalar.activation(h_full[:, m % 2, :], bank_h[m % 3][:, :], ACT.Silu)
                    nc.scalar.activation(h_hi[m // FK][:, m % FK, :], bank_h[m % 3][:, :], ACT.Silu).then_inc(h_hi_ready, 1)
                    if m >= FK or m % 2:
                        unit(w, AHEAD + unit_of(m))
                    if m in TURN_H:
                        turned(w + 1, TURN_H.index(m))
                for u in range(NU - 4, NU):
                    unit(w, AHEAD + u)
                    if u in TURN_W:
                        turned(w + 1, len(TURN_H) + TURN_W.index(u))
                act.wait_ge(cur_ready, w + 1)
                for i in range(BLK):
                    act.wait_ge(y_done, BLK * w + i + 1 + BLK)
                    if i == 0:
                        act.wait_ge(y_free, w + 1)
                    nc.scalar.activation(y_sb[:, i, :], bank_y[i][:, :], ACT.Copy, scale=gate[:, i:i + 1]).then_inc(y_ready, 1)

        @block.vector
        def _(dve):
            v = nc.vector
            steps = [0]

            def then(ins):
                steps[0] += 1
                ins.then_inc(route_step, 1)
                dve.wait_ge(route_step, steps[0])

            v.memset(eps_col[:], EPS).then_inc(eps2_ready, 1)
            for h, half in enumerate((range(0, B // 2), range(B // 2, B))):
                for b in half:
                    last = v.bn_stats(stats[:, b, :], acc[:, b, :])
                then(last)
                for b in half:
                    v.bn_aggr(mean_var[:, b, :], stats[:, b, :]).then_inc(mv2_ready, 1)
                dve.wait_ge(std2_ready, h + 1)
                then(v.reciprocal(rstd[:, half.start:half.stop], rstd[:, half.start:half.stop]))
                dve.wait_ge(mv2_ready, half.stop)
                for b in half:
                    v.tensor_scalar(xn2[:, b, :], acc[:, b, :], mean_var[:, b, 0:1], rstd[:, b:b + 1], ALU.subtract, ALU.mult).then_inc(xn2_ready, 1)
            dve.wait_ge(route_loaded, 16 * 8)
            v.tensor_copy(upper_r[:], upper[:])
            v.tensor_copy(ones_r[:], ones[:])
            v.memset(pos_tab[:, E:2 * E, :], -1.0)
            v.memset(items_f[:], 0.0)
            v.tensor_copy(row_tab[:, :, :, 0], token_row[:].unsqueeze(1).to_broadcast([S, NIT, B]))
            then(v.tensor_copy(row_tab[:, :, :, 1], ones[:, 0:1].unsqueeze(1).to_broadcast([S, NIT, B])))
            dve.wait_ge(logits_done, 1)
            then(v.tensor_copy(logits[:], bank_t[0:S, 0:B * E].rearrange("s (b e) -> s b e", e=E)))
            other = logits[:].unsqueeze(2).to_broadcast([S, B, E, E])
            own = logits[:].unsqueeze(3).to_broadcast([S, B, E, E])
            v.tensor_tensor(pair[:], other, own, ALU.is_gt)
            then(v.tensor_tensor(pair2[:], other, own, ALU.is_equal))
            then(v.tensor_tensor(pair2[:], pair2[:], before[:].unsqueeze(1).to_broadcast([S, B, E, E]), ALU.mult))
            then(v.tensor_tensor(pair[:], pair[:], pair2[:], ALU.add))
            then(v.tensor_reduce(rank[:], pair[:], AX_X, ALU.add))
            v.tensor_scalar(mask_r[:], rank[:], float(TOPK), None, ALU.is_lt).then_inc(mask_ready, 1)
            then(v.tensor_scalar(mask[:], rank[:], float(TOPK), None, ALU.is_lt))
            then(v.tensor_reduce(lmax[:], logits[:], AX_X, ALU.max))
            v.tensor_tensor(prob[:], logits[:], lmax[:].unsqueeze(2).to_broadcast([S, B, E]), ALU.subtract).then_inc(shifted_ready, 1)
            dve.wait_ge(exp2_ready, 1)
            then(v.tensor_tensor(prob[:], prob[:], mask[:], ALU.mult))
            then(v.tensor_reduce(psum_k[:], prob[:], AX_X, ALU.add))
            then(v.reciprocal(psum_k[:], psum_k[:]))
            then(v.tensor_tensor(gates[:], prob[:], psum_k[:].unsqueeze(2).to_broadcast([S, B, E]), ALU.mult))
            then(v.tensor_scalar(gates[:], gates[:], ffn_gate[0:S], None, ALU.mult))
            dve.wait_ge(pos_done, 1)
            then(v.tensor_scalar(posm[:], bank_t[0:S, B * E:2 * B * E].rearrange("s (b e) -> s b e", e=E), 1.0, None, ALU.add))
            then(v.tensor_tensor(posm[:], posm[:], mask[:], ALU.mult))
            v.tensor_copy(count[:], bank_t[:, 2 * B * E:2 * B * E + E])
            v.tensor_scalar(pos_tab[:, 0:E, :], posm[:].rearrange("s b e -> s e b"), -1.0, None, ALU.add)
            gates_by_expert = gates[:].rearrange("s b e -> s e b")
            then(v.tensor_copy(row_tab[:, 0:E, :, 2], gates_by_expert))
            then(v.tensor_tensor(row_tab[:, 0:E, :, 3], gates_by_expert, row_tab[:, 0:E, :, 2].bitcast(F32), ALU.subtract))
            dve.sem_inc(tables_ready, 1)

            def unit(w, u):
                dve.wait_ge(unit_hi, NU * w + u + 1)
                v.tensor_tensor(w_lo[:, u % RING, :], raw[:, u % RAW, :], w_hi[:, u % RING, :].bitcast(F32), ALU.subtract).then_inc(unit_lo, 1)

            def hot(n, b):
                dve.wait_ge(hot_used, B * n + b + 1)
                v.tensor_scalar(onehot[:, b % HOT, :], iota[:], pos_tab[:, bass.ds(n, 1), b], None, ALU.is_equal).then_inc(hot_ready, 1)

            def make_list(n):
                dve.wait_ge(hot_used, B * n + B + HOT)
                v.tensor_copy(lists[:], bank_t[:, 0:BLK * 4].rearrange("p (i c) -> p i c", c=4)).then_inc(list_step, 1)
                dve.wait_ge(list_step, 4 * n + 1)
                v.tensor_scalar(row_f[:], lists[:, :, 1], -1.0, 1.0, ALU.mult, ALU.add).then_inc(list_step, 1)
                dve.wait_ge(list_step, 4 * n + 2)
                v.tensor_tensor(row_f[:], row_f[:], pad_row[:], ALU.mult).then_inc(list_step, 1)
                dve.wait_ge(list_step, 4 * n + 3)
                v.tensor_tensor(idx_next[:], row_f[:], lists[:, :, 0], ALU.add).then_inc(idx_ready, 1)
                v.tensor_tensor(gate_next[:], lists[:, :, 2], lists[:, :, 3], ALU.add).then_inc(list_step, 1)

            def turned(n, i):
                dve.wait_ge(xT_hi_ready, BLK * n + i + 1)
                at = slice(i * P, (i + 1) * P)
                v.tensor_tensor(xT_lo[:, :, at], turn_bank(n, i)[:, :].rearrange("p (k s) -> p k s", k=DK), xT_hi[:, :, at].bitcast(F32),
                                ALU.subtract).then_inc(xT_ready, 1)

            dve.wait_ge(rows_stored, 64)
            for b in range(B):
                hot(0, b)
            make_list(0)
            then(v.tensor_scalar(ovf[:], count[:], float(CAP), None, ALU.is_gt))
            then(v.tensor_tensor(ovf_pair[0:S], before[:], ovf[0:S].unsqueeze(1).to_broadcast([S, E, E]), ALU.mult))
            then(v.tensor_reduce(ovf_at[0:S], ovf_pair[0:S], AX_X, ALU.add))
            then(v.tensor_tensor(sel[0:S], ovf_at[0:S].unsqueeze(1).to_broadcast([S, E, E]),
                                 expert_id[0:S].unsqueeze(2).to_broadcast([S, E, E]), ALU.is_equal))
            v.tensor_copy(items_f[0:S, 0:E], expert_id[0:S])
            then(v.tensor_tensor(sel[0:S], sel[0:S], ovf[0:S].unsqueeze(1).to_broadcast([S, E, E]), ALU.mult))
            pick = sel[0:S].unsqueeze(1).to_broadcast([S, B, E, E])
            v.tensor_tensor(pair[:], pick, posm[:].unsqueeze(2).to_broadcast([S, B, E, E]), ALU.mult)
            then(v.tensor_tensor(pair2[:], pick, gates[:].unsqueeze(2).to_broadcast([S, B, E, E]), ALU.mult))
            v.tensor_tensor(ovf_pair[0:S], sel[0:S], expert_id[0:S].unsqueeze(1).to_broadcast([S, E, E]), ALU.mult)
            v.tensor_reduce(n_ovf[:], ovf[:], AX_X, ALU.add)
            then(v.tensor_reduce(rank[:], pair[:], AX_X, ALU.add))
            v.tensor_reduce(items_f[0:S, E:2 * E], ovf_pair[0:S], AX_X, ALU.add)
            v.tensor_scalar(pos_tab[:, E:2 * E, :], rank[:].rearrange("s b q -> s q b"), -1.0 - CAP, None, ALU.add)
            then(v.tensor_scalar(n_items[:], n_ovf[0:1, :], float(E), None, ALU.add))
            v.tensor_copy(experts[:], items_f[0:1, :])
            then(v.tensor_reduce(gate_ovf[:].rearrange("s q b -> s b q"), pair2[:], AX_X, ALU.add))
            then(v.tensor_copy(row_tab[:, E:2 * E, :, 2], gate_ovf[:]))
            v.tensor_tensor(row_tab[:, E:2 * E, :, 3], gate_ovf[:], row_tab[:, E:2 * E, :, 2].bitcast(F32), ALU.subtract).then_inc(tables_ready, 1)
            for i in range(BLK):
                turned(0, i)
            dve.wait_ge(unit_lo, AHEAD)
            items = items_count(dve)
            with dve.Fori(0, items) as w:
                for m in range(2 * FK):
                    dve.wait_ge(h_hi_ready, 2 * FK * w + m + 1)
                    v.tensor_tensor(h_lo[m // FK][:, m % FK, :], h_full[:, m % 2, :], h_hi[m // FK][:, m % FK, :].bitcast(F32),
                                    ALU.subtract).then_inc(h_ready, 1)
                    if m >= FK or m % 2:
                        unit(w, AHEAD + unit_of(m))
                    if m == FK // 2:
                        dve.wait_ge(y_free, w + 1)
                        dve.wait_ge(list_step, 4 * w + 4)
                        v.tensor_copy(idx[:], idx_next[:])
                        v.tensor_copy(gate[:], gate_next[:]).then_inc(cur_ready, 1)
                    if m < B:
                        hot(w + 1, m)
                    if m == B + LAG:
                        dve.wait_ge(cur_ready, w + 1)
                        make_list(w + 1)
                    if m in TURN_H:
                        turned(w + 1, TURN_H.index(m))
                for u in range(NU - 4, NU):
                    unit(w, AHEAD + u)
                    if u in TURN_W:
                        turned(w + 1, len(TURN_H) + TURN_W.index(u))

        @block.tensor
        def _(pe):
            mm = nc.tensor.matmul
            def logits_of(b):
                pe.wait_ge(xn2T_ready, b + 1)
                for k in range(DK):
                    last = mm(bank_t[0:S, b * E:(b + 1) * E], xn2T[:, k, b * S:(b + 1) * S], router[:, k, :], start=(k == 0), stop=(k == DK - 1))
                return last

            pe.wait_ge(route_loaded, 16 * 8)
            for b in range(B):
                pe.wait_ge(xn2_ready, b + 1)
                for k in range(DK):
                    last = nc.tensor.transpose(bank_h[b % 3][:, k * S:(k + 1) * S], xn2[:, b, k * P:(k + 1) * P], ident[0:S, 0:S])
                last.then_inc(xn2T_done, 1)
                if b:
                    logits_of(b - 1)
            logits_of(B - 1).then_inc(logits_done, 1)
            pe.wait_ge(mask_ready, 1)
            pos = bank_t[0:S, B * E:2 * B * E]
            flat = mask_r[:].rearrange("s b e -> s (b e)")
            mm(pos, upper_r[:], flat, start=True, stop=False, skip_group_check=True)
            for d in range(1, B):
                mm(pos[:, d * E:], ones_r[:, 0:S], flat[:, 0:(B - d) * E], start=False, stop=(d == B - 1), skip_group_check=True)
            for b in range(B):
                last = mm(bank_t[:, 2 * B * E:2 * B * E + E], ones_r[:], mask_r[:, b, :], start=(b == 0), stop=(b == B - 1), skip_group_check=True)
            last.then_inc(pos_done, 1)
            pe.sem_inc(unit_used, AHEAD - 1)
            pe.sem_inc(y_done, BLK)
            pe.sem_inc(hot_used, HOT)

            def lists_of(n, b):
                pe.wait_ge(hot_ready, B * n + b + 1)
                for i in range(BLK):
                    last = mm(bank_t[:, 4 * i:4 * i + 4], onehot[:, b % HOT, i * P:(i + 1) * P],
                              row_tab[:, bass.ds(n, 1), b, :].rearrange("s o c -> s (o c)"),
                              start=(b == 0 and i == 0), stop=(b == B - 1), skip_group_check=True)
                last.then_inc(hot_used, 1)

            def turn(n, i):
                if i and turn_bank(n, i) is bank_t:
                    pe.wait_ge(xT_ready, BLK * n + i)
                pe.wait_ge(gathered[i], 16 * (n + 1))
                for k in range(DK):
                    last = nc.tensor.transpose(turn_bank(n, i)[:, k * P:(k + 1) * P], xg[:, i, k * P:(k + 1) * P], ident[:])
                last.then_inc(xT_done, 1)

            pe.wait_ge(tables_ready, 1)
            for b in range(B):
                lists_of(0, b)
            for i in range(BLK):
                turn(0, i)
            items = items_count(pe)
            with pe.Fori(0, items) as w:
                pe.wait_ge(xT_ready, BLK * w + BLK)
                for m in range(2 * FK):
                    layer2 = m >= FK
                    n = 2 * FK * w + m
                    u = unit_of(m)
                    pe.wait_ge(unit_lo, NU * w + u + 1)
                    if m >= 3:
                        pe.wait_ge(h_ready, n - 2)
                    kk = FK if layer2 else DK
                    for k in range(kk):
                        if m == FK:
                            pe.wait_ge(h_ready, 2 * FK * w + k + 1)
                        at = slice(k * P, k * P + P) if layer2 else slice(k * 2 * P + (m % 2) * P, k * 2 * P + (m % 2) * P + P)
                        src_hi = h_hi[0][:, k, :] if layer2 else xT_hi[:, k, :]
                        src_lo = h_lo[0][:, k, :] if layer2 else xT_lo[:, k, :]
                        last = three_pass(mm, bank_h[m % 3][:, :], w_hi[:, u % RING, at], w_lo[:, u % RING, at], src_hi, src_lo,
                                          k == 0, k == kk - 1)
                    last.then_inc(h_done, 1)
                    if LAG <= m < B + LAG:
                        lists_of(w + 1, m - LAG)
                    if m in TURN_H:
                        turn(w + 1, TURN_H.index(m))
                for u in range(12, NU):
                    pe.wait_ge(unit_lo, NU * w + u + 1)
                    for i in range(BLK):
                        for c in range(2):
                            k = 2 * (u - 12) + c
                            if i == 0:
                                pe.wait_ge(h_ready, 2 * FK * w + FK + k + 1)
                            at = slice(c * D, (c + 1) * D)
                            tok = slice(i * P, (i + 1) * P)
                            last = three_pass(mm, bank_y[i][:, :], h_hi[1][:, k, tok], h_lo[1][:, k, tok], w_hi[:, u % RING, at], w_lo[:, u % RING, at],
                                              k == 0, k == FK - 1)
                        if u == NU - 1:
                            last.then_inc(y_done, 1)
                    if u < NU - 1:
                        last.then_inc(unit_used, 1)
                    if u in TURN_W:
                        turn(w + 1, len(TURN_H) + TURN_W.index(u))


def rope_tables(length, dim):
    inv = (np.float32(1.0) / np.float32(10000.0) ** (np.arange(0, dim, 2, dtype=np.float32) / np.float32(dim))).astype(np.float32)
    f = np.arange(length, dtype=np.float32)[:, None] * inv[None, :]
    return np.repeat(np.cos(f), 2, axis=-1), np.repeat(np.sin(f), 2, axis=-1)


def latent_order():
    lower = np.arange(DQ // 2).reshape(QC, P // 2)
    return np.concatenate([lower, lower + DQ // 2], axis=1).reshape(-1)


def constants():
    cq, sq = rope_tables(S, DQ)
    sq = sq.copy()
    sq[:, :DQ // 2] *= -1
    order = latent_order()
    ck, sk = rope_tables(L, DC)
    sk = sk.copy()
    sk[:, :DC // 2] *= -1
    return {
        "cos_q": cq[:, order].T.reshape(QC, P, S).transpose(1, 0, 2), "sin_q": sq[:, order].T.reshape(QC, P, S).transpose(1, 0, 2),
        "cos_k": ck.reshape(LC, LP, DC).transpose(1, 0, 2), "sin_k": sk.reshape(LC, LP, DC).transpose(1, 0, 2),
        "ident": np.eye(P, dtype=np.float32),
        "iota": np.arange(CAP, dtype=np.float32), "before": np.broadcast_to(np.tri(E, E, -1, dtype=np.float32), (S, E, E)),
        "upper": np.tri(S, S, -1, dtype=np.float32).T, "ones": np.ones((S, P), np.float32),
        "token_row": (np.arange(S, dtype=np.float32)[:, None] + np.float32(S) * np.arange(B, dtype=np.float32)[None, :]),
        "expert_id": np.broadcast_to(np.arange(E, dtype=np.float32), (P, E)),
        "pad_row": np.float32(B * S) + np.arange(CAP, dtype=np.float32).reshape(BLK, P).T,
    }


def layouts(x):
    order = latent_order()
    return {
        "x": x["x"].reshape(B * S, D), "ctx": x["ctx_512"], "g_xattn": x["g_xattn"], "g_ffn": x["g_ffn"],
        "wq": x["L0_xattn_Wq"].reshape(H, KH, DK, P).transpose(0, 3, 2, 1),
        "wc": x["L0_xattn_w_kc_q"][:, :, order],
        "wqr": x["L0_xattn_W_qr"].transpose(0, 2, 1)[:, :, order],
        "wkr": x["L0_xattn_W_kr"].transpose(0, 2, 1),
        "wkv": x["L0_xattn_w_kc_kv"],
        "wo": x["L0_xattn_Wo"].T.reshape(H, KH, D),
        "router": x["L0_ffn_router_w"].reshape(DK, P, E).transpose(1, 0, 2),
        "units": np.concatenate([
            x["L0_ffn_w1"].reshape(E, DK, P, 4, 2 * P).transpose(0, 3, 2, 1, 4).reshape(E, 4, P, UNIT),
            x["L0_ffn_w2"].reshape(E, FK, P, FK, P).transpose(0, 3, 2, 1, 4).reshape(E, FK, P, UNIT),
            x["L0_ffn_w3"].reshape(E, 4, 2, P, D).transpose(0, 1, 3, 2, 4).reshape(E, 4, P, UNIT)], axis=1),
    }


def program(nc, io, out):
    with nc.sbuf_tensor("acc", [S, B, D], F32) as acc, nc.sbuf_tensor("ident", [P, P], F32) as ident, \
            nc.sbuf_tensor("ffn_gate", [P, 1], F32) as ffn_gate:
        keep = {"acc": acc, "ident": ident, "ffn_gate": ffn_gate}
        build_attention(nc, io, keep)
        build_experts(nc, io, out, keep)


def kernel(**inputs):
    import concourse.bacc as bacc
    from concourse.bass_utils import run_bass_kernel_spmd as run

    x = {name: np.asarray(a) for name, a in inputs.items()}
    nc = bacc.Bacc("TRN2", target_bir_lowering=False, num_devices=1)
    arrays, io = {}, {}
    for name, a in (layouts(x) | constants()).items():
        arrays["in_" + name] = np.ascontiguousarray(a)
        io[name] = nc.dram_tensor("in_" + name, a.shape, F32, kind="ExternalInput").ap()
    out = nc.dram_tensor("out_x", [ROWS, D], F32, kind="ExternalOutput").ap()
    program(nc, io, out)
    r = run(nc, [arrays], core_ids=[0])
    return r.results[0]["out_x"][:B * S].reshape(B, S, D)
```
